# Optimizing a Trainium2 kernel written in Bass

```python
import numpy as np
import jax
import jax.numpy as jnp

def _softmax(x, axis=-1):
    return jax.nn.softmax(x, axis=axis)

def _gelu(x):
    return jax.nn.gelu(x, approximate=True)

def _silu(x):
    return jax.nn.silu(x)

def _sigmoid(x):
    return jax.nn.sigmoid(x)

def _layernorm(x, axis=-1, eps=1e-05):
    m = jnp.mean(x, axis=axis, keepdims=True)
    v = jnp.var(x, axis=axis, keepdims=True)
    return (x - m) / jnp.sqrt(v + eps)

def _scatter_add(tgt, idx, src, axis=0):
    return tgt.at[idx].add(src)

def _segment_sum(src, seg, n):
    return jax.ops.segment_sum(src, seg, n)
kernel_name = 'mk_gps_d1_gnn_r32_f3f986'

def setup_inputs(seed: int=0):
    np.random.seed(seed)
    _w = jnp.asarray

    def _rec_inputs():
        import jax
        import jax.numpy as jnp
        _gk = jax.random.key(seed)
        x = -0.0002117 + 1 * jax.random.normal(jax.random.fold_in(_gk, 1), (3125, 256), jnp.float32)
        _s = jax.random.randint(jax.random.fold_in(_gk, 2), (25000,), 0, 3125, jnp.int32)
        _d = jax.random.randint(jax.random.fold_in(_gk, 3), (25000,), 0, 3125, jnp.int32)
        _loop = jnp.arange(3125, dtype=jnp.int32)
        src = jnp.concatenate([_s, _d, _loop])
        dst = jnp.concatenate([_d, _s, _loop])
        _o = jnp.argsort(dst, stable=True)
        src = src[_o]
        dst = dst[_o]
        edge_weight = jax.random.uniform(jax.random.fold_in(_gk, 12), (53125,), jnp.float32, 0.0, 1)
        return (x, src, dst, edge_weight)
    x, src, dst, edge_weight = _rec_inputs()

    def _L0_gnn_setup():
        import jax, jax.numpy as jnp
        import numpy as np
        N_NODES = 3125
        N_EDGES = 100000
        N_IN = 256
        N_OUT = 256
        key = jax.random.key(seed)
        k1, k2, k3, k4, k5 = jax.random.split(key, 5)
        x = jax.random.normal(k1, (N_NODES, N_IN), dtype=jnp.float32)
        W = jax.random.normal(k2, (N_IN, N_OUT), dtype=jnp.float32) * (1.0 / np.sqrt(N_IN))
        edge_row = jax.random.randint(k3, (N_EDGES,), 0, N_NODES, dtype=jnp.int32)
        edge_col = jax.random.randint(k4, (N_EDGES,), 0, N_NODES, dtype=jnp.int32)
        edge_val = jax.random.uniform(k5, (N_EDGES,), dtype=jnp.float32)
        return {'x': x, 'W': W, 'edge_row': edge_row, 'edge_col': edge_col, 'edge_val': edge_val}
    _L0_gnn_all = _L0_gnn_setup()
    _L0_gnn_in = {k: v for k, v in _L0_gnn_all.items() if k in ('W',)}
    del _L0_gnn_all

    def _L0_mix_setup():
        import jax, jax.numpy as jnp
        import numpy as np
        HEADS = 8
        DIM_HEAD = 32
        SCALE = DIM_HEAD ** (-0.5)
        EPS = 1e-05

        def _layernorm_gamma(x, gamma):
            mu = jnp.mean(x, axis=-1, keepdims=True)
            var = jnp.var(x, axis=-1, keepdims=True)
            return (x - mu) * jax.lax.rsqrt(var + EPS) * gamma
        key = jax.random.key(seed)
        k1, k2, k3 = jax.random.split(key, 3)
        B, N, D = (8, 512, 256)
        hidden = HEADS * DIM_HEAD
        x = jax.random.normal(k1, (B, N, D), dtype=jnp.float32)
        Wqkv = jax.random.normal(k2, (D, 3 * hidden), dtype=jnp.float32) * D ** (-0.5)
        Wout = jax.random.normal(k3, (hidden, D), dtype=jnp.float32) * hidden ** (-0.5)
        gamma = jnp.ones((D,), dtype=jnp.float32)
        return {'x': x, 'Wqkv': Wqkv, 'Wout': Wout, 'gamma': gamma}
    _L0_mix_all = _L0_mix_setup()
    _L0_mix_in = {k: v for k, v in _L0_mix_all.items() if k in ('Wqkv', 'Wout', 'gamma')}
    del _L0_mix_all

    def _L0_ffn_setup():
        import jax, jax.numpy as jnp
        import numpy as np
        N_EXPERTS = 8
        TOP_K = 2
        key = jax.random.key(seed)
        ks = jax.random.split(key, 5)
        B, T, C, E, H = (8, 64, 256, 8, 682)
        scale = 1.0 / np.sqrt(C)
        return {'x': jax.random.normal(ks[0], (B, T, C), dtype=jnp.float32), 'router_w': jax.random.normal(ks[1], (E, C), dtype=jnp.float32) * scale, 'w1': jax.random.normal(ks[2], (E, H, C), dtype=jnp.float32) * scale, 'w2': jax.random.normal(ks[3], (E, C, H), dtype=jnp.float32) * (1.0 / np.sqrt(H)), 'w3': jax.random.normal(ks[4], (E, H, C), dtype=jnp.float32) * scale}
    _L0_ffn_all = _L0_ffn_setup()
    _L0_ffn_in = {k: v for k, v in _L0_ffn_all.items() if k in ('router_w', 'w1', 'w2', 'w3')}
    del _L0_ffn_all
    return {'x': x, 'src': src, 'dst': dst, 'edge_weight': edge_weight, 'L0_gnn_W': _L0_gnn_in['W'], 'L0_mix_Wqkv': _L0_mix_in['Wqkv'], 'L0_mix_Wout': _L0_mix_in['Wout'], 'L0_mix_gamma': _L0_mix_in['gamma'], 'L0_ffn_router_w': _L0_ffn_in['router_w'], 'L0_ffn_w1': _L0_ffn_in['w1'], 'L0_ffn_w2': _L0_ffn_in['w2'], 'L0_ffn_w3': _L0_ffn_in['w3']}

def reference(x, src, dst, edge_weight, L0_gnn_W, L0_mix_Wqkv, L0_mix_Wout, L0_mix_gamma, L0_ffn_router_w, L0_ffn_w1, L0_ffn_w2, L0_ffn_w3):
    import jax
    import jax.numpy as jnp

    def _L0_gnn_ref(x, W, edge_row, edge_col, edge_val):
        import jax, jax.numpy as jnp
        import numpy as np
        N_NODES = 3125
        N_EDGES = 100000
        N_IN = 256
        N_OUT = 256
        support = jnp.matmul(x, W)
        msgs = support[edge_col] * edge_val[:, None]
        out = jax.ops.segment_sum(msgs, edge_row, num_segments=N_NODES)
        return out

    def _L0_mix_ref(x, Wqkv, Wout, gamma):
        import jax, jax.numpy as jnp
        import numpy as np
        HEADS = 8
        DIM_HEAD = 32
        SCALE = DIM_HEAD ** (-0.5)
        EPS = 1e-05

        def _layernorm_gamma(x, gamma):
            mu = jnp.mean(x, axis=-1, keepdims=True)
            var = jnp.var(x, axis=-1, keepdims=True)
            return (x - mu) * jax.lax.rsqrt(var + EPS) * gamma
        B, N, D = x.shape
        qkv = x @ Wqkv
        q, k, v = jnp.split(qkv, 3, axis=-1)

        def to_heads(t):
            return t.reshape(B, N, HEADS, DIM_HEAD).transpose(0, 2, 1, 3)
        q, k, v = map(to_heads, (q, k, v))
        q = jax.nn.softmax(q, axis=-1) * SCALE
        k = jax.nn.softmax(k, axis=2)
        context = jnp.einsum('bhnd,bhne->bhde', k, v)
        out = jnp.einsum('bhde,bhnd->bhne', context, q)
        out = out.transpose(0, 2, 1, 3).reshape(B, N, HEADS * DIM_HEAD)
        out = out @ Wout
        return _layernorm_gamma(out, gamma)

    def _L0_ffn_ref(x, router_w, w1, w2, w3):
        import jax, jax.numpy as jnp
        import numpy as np
        N_EXPERTS = 8
        TOP_K = 2
        B, T, C = x.shape
        flat = x.reshape(-1, C)
        logits = flat @ router_w.T
        probs = jax.nn.softmax(logits, axis=-1)
        topk_probs, topk_idx = jax.lax.top_k(probs, TOP_K)
        topk_probs = topk_probs / (jnp.sum(topk_probs, axis=-1, keepdims=True) + 1e-09)
        onehot = jax.nn.one_hot(topk_idx, N_EXPERTS, dtype=flat.dtype)
        gates = jnp.einsum('nk,nke->ne', topk_probs, onehot)
        h1 = jnp.einsum('nc,ehc->neh', flat, w1)
        h3 = jnp.einsum('nc,ehc->neh', flat, w3)
        h = jax.nn.silu(h1) * h3
        y = jnp.einsum('neh,ech->nec', h, w2)
        out = jnp.einsum('ne,nec->nc', gates, y)
        return out.reshape(B, T, C)
    xn = _layernorm(x, axis=-1)
    x = x + _L0_gnn_ref(xn, L0_gnn_W, src, dst, edge_weight) + _L0_mix_ref(xn[None], L0_mix_Wqkv, L0_mix_Wout, L0_mix_gamma)[0]
    x = x + _L0_ffn_ref(_layernorm(x, axis=-1)[None], L0_ffn_router_w, L0_ffn_w1, L0_ffn_w2, L0_ffn_w3)[0]
    return x

_drawn_inputs = setup_inputs


def setup_inputs(seed=0):
    import zlib

    import numpy as np

    out = dict(_drawn_inputs(seed))
    spreads = {'L0_mix_gamma': (1.0, 0.2)}
    factors = {}
    for name, (base, spread) in spreads.items():
        noise = np.random.default_rng([zlib.crc32(name.encode()), seed]).standard_normal(out[name].shape)
        drawn = base * np.exp(spread * noise) if base else spread * noise
        out[name] = jnp.asarray(drawn.astype(out[name].dtype))
    for name, factor in factors.items():
        out[name] = (out[name] * factor).astype(out[name].dtype)
    return out
```

```python
import concourse.bass as bass
from concourse import mybir
from contextlib import ExitStack, contextmanager


def gps_layer_program(nc, x, src, dst, edge_weight, w_gnn, w_qkv, w_out, gamma, w_router, w_up, w_down,
                      x_out, support_table, edge_table, token_table, expert_out):
    f32, i32, u8 = mybir.dt.float32, mybir.dt.int32, mybir.dt.uint8
    ALU, ACT, AX = mybir.AluOpType, mybir.ActivationFunctionType, mybir.AxisListType

    L = 128
    N, D = x.shape
    T = 25
    P = N // T
    E = src.shape[0]
    C = E // P
    DC = D // L
    HEADS, DH = 8, 32
    HPC = L // DH
    XP = w_router.shape[1]
    H = w_up.shape[3] // 2
    HB = H // 2
    HC = -(-H // L)
    HL = H - (HC - 1) * L
    EPS = 1e-05
    SCALE = DH ** -0.5
    ROUND = 1.5 * 2.0 ** 23

    GU = 8
    GTURNS = -(-((E + T * (L - 1)) // L) // GU)
    NCH = GTURNS * GU
    NBLK = (2 * N + XP * (L - 1)) // L
    SA, SB_ = 9, 8
    SU = SA + SB_
    STURNS = C // SU
    QK = 4
    RING = 5
    assert STURNS * SU == C and P * T == N and P * C == E and NBLK % 2 == 0 and NBLK >= 6

    ctx = ExitStack()
    with ctx:
        def sb(name, shape, dt=f32):
            return ctx.enter_context(nc.sbuf_tensor(name, shape, dt))

        def sem(name):
            return ctx.enter_context(nc.semaphore(name))

        acc = sb("acc", [P, T, D])
        norm_all = sb("norm", [L, T * D])
        norm = norm_all[0:P, :].rearrange("p (t d) -> p t d", d=D)
        gbuf = norm_all[:, 0:GU * D].rearrange("p (k n) -> p k n", k=GU)
        onehot = norm_all[:, GU * D:GU * (D + P)].rearrange("p (k n) -> p k n", k=GU)
        accf = acc[:, :, :].rearrange("p t d -> p (t d)")
        normf = norm_all[0:P, :]
        ident = sb("ident", [L, L])
        upper = sb("upper", [P, P])
        ones = sb("ones", [P, L])
        lane_no = sb("lane_no", [L, P])
        chunk_tile = sb("chunk_tile", [1, NCH], i32)
        block_expert = sb("block_expert", [1, NBLK], i32)
        small = sb("small", [L, 640])

        WUP, WDN = XP * DC * 2 * H, XP * HC * D
        arena = sb("arena", [L, WUP + WDN])
        wup = arena[:, 0:WUP]
        wdn = arena[:, WUP:WUP + WDN]
        at = [0]

        def carve(cols, rows=L):
            a = at[0]
            at[0] += cols
            assert at[0] <= WUP + WDN
            return arena[0:rows, a:a + cols]

        src_i, dst_i = carve(C, P).bitcast(i32), carve(C, P).bitcast(i32)
        wgt = carve(C, P)
        tile_of = carve(C, P)
        row_of = carve(C, P)
        rank = carve(C, P)
        tmp = carve(C, P)
        tmp2 = carve(C, P)
        mask = carve(C // 4 + 1, P).bitcast(u8)[:, 0:C]
        zeros = carve(max(NCH * 3, 1024))
        chunk_no = carve(NCH, 1)
        chunk_acc = carve(NCH, 1)
        wqkvg = carve(DC * 4 * D).rearrange("p (c n) -> p c n", c=DC)
        wout_sb = carve(DC * D).rearrange("p (c n) -> p c n", c=DC)
        gamma_sb = carve(D, P)
        xn = carve(D, P)
        xnT = carve(DC * P).rearrange("p (c n) -> p c n", c=DC)
        qT = carve(DC * P).rearrange("p (c n) -> p c n", c=DC)
        Q = carve(T * D, P)
        K = carve(T * D, P)
        V = carve(T * D, P)
        kmax = carve(D, P)
        kshift = carve(D, P)
        kmaxb = carve(DC * P).rearrange("p (c n) -> p c n", c=DC)
        ctxT = carve(DC * L).rearrange("p (c n) -> p c n", c=DC)
        mix_w = carve(DC * D).rearrange("p (c n) -> p c n", c=DC)
        y_ring = arena[0:P, 0:RING * 2 * D].rearrange("p (r n) -> p r n", r=RING * 2)

        WORK = 2 * D + DC * L + 3 * H + HC * L + 2 * D
        work = sb("work", [L, WORK])
        rec_in = work[:, 0:NCH * 3]
        gidx = work[:, NCH * 3:NCH * 4].bitcast(i32)
        rec = work[0:P, NCH * 4:NCH * 4 + 3 * C]
        slot_i = work[0:P, NCH * 4 + 3 * C:NCH * 4 + 4 * C].bitcast(i32)
        wat = [0]

        def wcarve(cols):
            a = wat[0]
            wat[0] += cols
            assert wat[0] <= WORK
            return work[:, a:a + cols]

        X = [wcarve(D), wcarve(D)]
        XT = wcarve(DC * L).rearrange("p (c n) -> p c n", c=DC)
        silu = wcarve(H).rearrange("p (a n) -> p a n", a=2)
        G = [wcarve(H), wcarve(H)]
        GT = wcarve(HC * L).rearrange("p (c n) -> p c n", c=HC)
        Y = [wcarve(D), wcarve(D)]

        stage_slot = [sb("stage_slot0", [P, SA], i32), sb("stage_slot1", [P, SB_], i32)]
        stage_rec = [sb("stage_rec0", [P, SA * 3]), sb("stage_rec1", [P, SB_ * 3])]
        stage_gidx = [sb("stage_gidx0", [L, GU // 2], i32), sb("stage_gidx1", [L, GU // 2], i32)]
        pair_slot = sb("pair_slot", [P, 2, T], i32)

        so = [0]

        def s_carve(cols, rows=L):
            a = so[0]
            so[0] += cols
            assert so[0] <= 640
            return small[0:rows, a:a + cols]

        tile_no = s_carve(T)
        count = s_carve(T, P)
        first_slot = s_carve(T, P)
        blocks = s_carve(T)
        blocks_to = s_carve(T)
        stats6 = s_carve(6 * T, P)
        stats = stats6.rearrange("p (t s) -> p t s", s=6)
        mean = s_carve(T, P)
        spread = s_carve(T, P)
        rstd = s_carve(T, P)
        qmax = s_carve(HEADS, P)
        qsum = s_carve(HEADS, P)
        qrec = s_carve(HEADS, P)
        kneg = s_carve(DC)
        krec = s_carve(DC)
        wr_sb = s_carve(DC * XP).rearrange("p (c n) -> p c n", c=DC)
        gate = s_carve(2 * T, P).rearrange("p (k t) -> p k t", k=2)
        block_no = s_carve(NBLK, 1)
        block_acc = s_carve(NBLK, 1)

        TX = T * XP
        rw = work[0:P, 0:7 * TX + 4 * T]

        def r3(n):
            return rw[:, n * TX:(n + 1) * TX].rearrange("p (t e) -> p t e", e=XP)

        probs, key, first, second, both, cum, place = (r3(n) for n in range(7))
        r1 = [rw[:, 7 * TX + n * T:7 * TX + (n + 1) * T] for n in range(4)]
        rxT = work[:, 7 * TX + 4 * T:7 * TX + 4 * T + 2 * DC * P].rearrange("p (k c n) -> p k c n", k=2, c=DC)
        rxn = work[0:P, 7 * TX + 4 * T + 2 * DC * P:7 * TX + 4 * T + 2 * DC * P + 2 * D]\
            .rearrange("p (k n) -> p k n", k=2)
        expert_rev = sb("expert_rev", [P, XP])

        ps = ctx.enter_context(nc.psum_tensor("ps", [L, 8, 512], f32))

        s_edges = sem("s_edges")
        s_x = sem("s_x")
        s_x2 = sem("s_x2")
        s_w = sem("s_w")
        s_zfill = sem("s_zfill")
        s_recs = sem("s_recs")
        s_support_out = sem("s_support_out")
        s_wup = sem("s_wup")
        s_const = sem("s_const")
        s_pool = sem("s_pool")
        s_dve = sem("s_dve")
        s_act = sem("s_act")
        count_ready = sem("count_ready")
        base_ready = sem("base_ready")
        slots_ready = sem("slots_ready")
        zeros_ready = sem("zeros_ready")
        scattered = [sem("scattered0"), sem("scattered1")]
        var_ready = sem("var_ready")
        std_ready = sem("std_ready")
        xn_ready = sem("xn_ready")
        xn_free = sem("xn_free")
        xnT_psum = sem("xnT_psum")
        xnT_ready = sem("xnT_ready")
        proj_ready = sem("proj_ready")
        proj_free_act = sem("proj_free_act")
        proj_free_dve = sem("proj_free_dve")
        q_shifted = sem("q_shifted")
        q_exped = sem("q_exped")
        q_ready = sem("q_ready")
        support_ready = sem("support_ready")
        kmaxT_ready = sem("kmaxT_ready")
        kmaxb_ready = sem("kmaxb_ready")
        kshift_psum = sem("kshift_psum")
        kshift_ready = sem("kshift_ready")
        k_shifted = sem("k_shifted")
        k_exped = sem("k_exped")
        ctx_ready = sem("ctx_ready")
        ctxT_ready = sem("ctxT_ready")
        mixw_psum = sem("mixw_psum")
        mixw_ready = sem("mixw_ready")
        q_staged = sem("q_staged")
        qT_psum = sem("qT_psum")
        qT_ready = sem("qT_ready")
        mix_psum = sem("mix_psum")
        mix_copied = sem("mix_copied")
        arena_free = sem("arena_free")
        gidx_ready = sem("gidx_ready")
        map_ready = sem("map_ready")
        gathered = [sem(f"gathered{k}") for k in range(GU)]
        onehot_ready = sem("onehot_ready")
        chunk_summed = sem("chunk_summed")
        chunk_added = sem("chunk_added")
        norm_ready = sem("norm_ready")
        rT_psum = sem("rT_psum")
        rT_ready = sem("rT_ready")
        logits_ready = sem("logits_ready")
        pair_count_ready = sem("pair_count_ready")
        pair_base_ready = sem("pair_base_ready")
        pair_slots_ready = sem("pair_slots_ready")
        expert_map_ready = sem("expert_map_ready")
        tokens_out = sem("tokens_out")
        x_loaded = [sem("x_loaded0"), sem("x_loaded1")]
        xt_psum = sem("xt_psum")
        xt_ready = sem("xt_ready")
        h_ready = sem("h_ready")
        silu_ready = sem("silu_ready")
        g_ready = sem("g_ready")
        gT_psum = sem("gT_psum")
        gT_act = sem("gT_act")
        gT_dve = sem("gT_dve")
        y_psum = sem("y_psum")
        y_ready = sem("y_ready")
        y_stored = [sem("y_stored0"), sem("y_stored1")]
        rows_back = [sem(f"rows_back{r}") for r in range(RING)]
        rows_added = sem("rows_added")
        s_out = sem("s_out")
        s_idle = sem("s_idle")

        def apart(eng):
            eng.sem_inc(s_idle, 1)

        class Steps:

            def __init__(self, eng, s):
                self.eng, self.s, self.n = eng, s, 0

            def mark(self, ins):
                ins.then_inc(self.s, 1)
                self.n = self.n + 1
                return self.n

            def wait(self):
                self.eng.wait_ge(self.s, self.n)

            def link(self, ins):
                self.mark(ins)
                self.wait()

            def link_apart(self, ins):
                self.link(ins)
                apart(self.eng)

            @contextmanager
            def loop(self, start, end, per):
                base = self.n
                with self.eng.Fori(start, end) as i:
                    self.n = base + (i - start) * per
                    yield i
                self.n = base + (end - start) * per

        block = ctx.enter_context(nc.Block())

        support_rows = support_table.rearrange("(p t) d -> p (t d)", t=T)
        edge_rows = edge_table.rearrange("(q c) r -> q (c r)", c=NCH)
        x_rows = x.rearrange("(p t) d -> p (t d)", t=T)
        out_rows = x_out.rearrange("(p t) d -> p (t d)", t=T)
        SPLIT = P // 16 * 16

        @block.sync
        def _(sp):
            sp.dma_start(src_i, src.rearrange("(p c) -> p c", c=C)).then_inc(s_edges, 16)
            sp.dma_start(dst_i, dst.rearrange("(p c) -> p c", c=C)).then_inc(s_edges, 16)
            sp.dma_start(wgt, edge_weight.rearrange("(p c) -> p c", c=C)).then_inc(s_edges, 16)
            sp.dma_start(accf[0:SPLIT], x_rows[0:SPLIT]).then_inc(s_x, 16)
            sp.dma_start(accf[SPLIT:P], x_rows[SPLIT:P]).then_inc(s_x2, 16)
            sp.dma_start(wqkvg[:, :, 0:D], w_gnn.rearrange("(c p) n -> p c n", p=L)).then_inc(s_w, 16)
            wq = w_qkv.rearrange("(c p) n -> p c n", p=L)
            sp.dma_start(wqkvg[:, :, D:2 * D], wq[:, :, 2 * D:3 * D]).then_inc(s_w, 16)
            sp.dma_start(wqkvg[:, :, 2 * D:4 * D], wq[:, :, 0:2 * D]).then_inc(s_w, 16)
            sp.dma_start(wout_sb, w_out.rearrange("(c p) n -> p c n", p=L)).then_inc(s_w, 16)
            sp.dma_start(wr_sb, w_router.rearrange("(c p) n -> p c n", p=L)).then_inc(s_w, 16)
            sp.dma_start(gamma_sb, gamma).then_inc(s_w, 16)
            sp.wait_ge(zeros_ready, 1)
            sp.dma_start(edge_rows, zeros[:, 0:NCH * 3]).then_inc(s_zfill, 16)
            fill = token_table.rearrange("(p a) d -> p (a d)", p=L).rearrange("p (m n) -> p m n", n=1024)
            for m in range(NBLK * D // 1024):
                sp.dma_start(fill[:, m, :], zeros[:, 0:1024]).then_inc(s_zfill, 16)
            sp.wait_ge(support_ready, T)
            sp.dma_start(support_rows[0:SPLIT], normf[0:SPLIT]).then_inc(s_support_out, 16)
            sp.dma_start(support_rows[SPLIT:P], normf[SPLIT:P]).then_inc(s_support_out, 16)
            sp.wait_ge(arena_free, 1)
            sp.wait_ge(s_zfill, 16 * (1 + NBLK * D // 1024))
            for e in range(XP):
                n = DC * 2 * H
                sp.dma_start(wup[:, e * n:(e + 1) * n], w_up[:, e, :, :].rearrange("p c n -> p (c n)"))\
                  .then_inc(s_wup, 16)
                n = HC * D
                sp.dma_start(wdn[:, e * n:(e + 1) * n], w_down[:, e, :, :].rearrange("p c n -> p (c n)"))\
                  .then_inc(s_wup, 16)
            sp.wait_ge(scattered[0], 16 * SA * STURNS)
            sp.wait_ge(scattered[1], 16 * SB_ * STURNS)
            sp.dma_start(rec_in, edge_rows).then_inc(s_recs, 16)

            def load(j, k):
                sp.dma_start(X[k], token_table[bass.ds(j * L, L), :]).then_inc(x_loaded[k], 16)

            def store(j, k):
                sp.wait_ge(y_ready, j + 1)
                sp.dma_start(expert_out[bass.ds(j * L, L), :], Y[k]).then_inc(y_stored[k], 16)

            sp.wait_ge(tokens_out, 16 * 2 * T)
            sp.wait_ge(chunk_added, QK + NCH)
            load(0, 0)
            load(1, 1)
            with sp.Fori(0, NBLK // 2 - 1) as i:
                for k in range(2):
                    sp.wait_ge(xt_psum, 2 * i + k + 1)
                    load(2 * i + 2 + k, k)
                    store(2 * i + k, k)
            store(NBLK - 2, 0)
            store(NBLK - 1, 1)
            for r in range(T // RING):
                sp.wait_ge(rows_added, RING * (r + 1))
                cols = slice(r * RING * D, (r + 1) * RING * D)
                sp.dma_start(out_rows[0:SPLIT, cols], accf[0:SPLIT, cols]).then_inc(s_out, 16)
                sp.dma_start(out_rows[SPLIT:P, cols], accf[SPLIT:P, cols]).then_inc(s_out, 16)
            sp.wait_ge(s_out, 16 * 2 * (T // RING))

        @block.gpsimd
        def _(pool):
            steps = Steps(pool, s_pool)
            pool.iota(tile_no, [[1, T]], base=0, channel_multiplier=0,
                      allow_small_or_imprecise_dtypes=True).then_inc(s_const, 1)
            steps.mark(pool.memset(upper[:], 1.0))
            steps.mark(pool.memset(ident[:], 0.0))
            steps.wait()
            pool.affine_select(out=upper[:], in_=upper[:], compare_op=ALU.is_gt, fill=0.0, base=0,
                               pattern=[[1, P]], channel_multiplier=-1).then_inc(s_const, 1)
            pool.affine_select(out=ident[:], in_=ident[:], compare_op=ALU.not_equal, fill=1.0, base=0,
                               pattern=[[-1, L]], channel_multiplier=1).then_inc(s_const, 1)
            pool.memset(ones[:], 1.0).then_inc(s_const, 1)
            pool.iota(lane_no[:], [[1, P]], base=0, channel_multiplier=0,
                      allow_small_or_imprecise_dtypes=True).then_inc(s_const, 1)
            pool.iota(chunk_no, [[1, NCH]], base=0, channel_multiplier=0,
                      allow_small_or_imprecise_dtypes=True).then_inc(s_const, 1)
            pool.iota(block_no, [[1, NBLK]], base=0, channel_multiplier=0,
                      allow_small_or_imprecise_dtypes=True).then_inc(s_const, 1)
            pool.iota(expert_rev[:], [[-1, XP]], base=XP, channel_multiplier=0,
                      allow_small_or_imprecise_dtypes=True).then_inc(s_const, 1)
            pool.memset(zeros, 0.0).then_inc(zeros_ready, 1)

            pool.wait_ge(slots_ready, 2)
            pool.wait_ge(s_zfill, 16 * (1 + NBLK * D // 1024))

            def scatter_half(i, h, first):
                n, at0 = (SA, 0) if h == 0 else (SB_, SA)
                if not first:
                    pool.wait_ge(scattered[h], 16 * n * i)
                steps.mark(pool.tensor_copy(stage_slot[h][:], slot_i[:, bass.ds(i * SU + at0, n)]))
                steps.mark(pool.tensor_copy(stage_rec[h][:], rec[:, bass.ds((i * SU + at0) * 3, n * 3)]))
                steps.wait()
                apart(pool)
                for c in range(n):
                    pool.indirect_dma_start(
                        out=edge_table, out_offset=bass.IndirectOffsetOnAxis(ap=stage_slot[h][:, c:c + 1], axis=0),
                        in_=stage_rec[h][:, 3 * c:3 * c + 3], in_offset=None).then_inc(scattered[h], 16)

            for h in range(2):
                scatter_half(0, h, True)
            with steps.loop(1, STURNS, 4) as i:
                for h in range(2):
                    scatter_half(i, h, False)

            pool.wait_ge(gidx_ready, 1)
            pool.wait_ge(s_support_out, 32)
            with steps.loop(0, GTURNS, 2) as i:
                for h in range(2):
                    top = GU // 2 * (h + 1)
                    pool.wait_ge(chunk_summed, i * GU + top)
                    steps.link_apart(pool.tensor_copy(stage_gidx[h][:], gidx[:, bass.ds(i * GU + GU // 2 * h, GU // 2)]))
                    for k in range(GU // 2 * h, top):
                        pool.indirect_dma_start(
                            out=gbuf[:, k, :], out_offset=None, in_=support_table,
                            in_offset=bass.IndirectOffsetOnAxis(ap=stage_gidx[h][:, k % 4:k % 4 + 1], axis=0))\
                            .then_inc(gathered[k], 16)

            pool.wait_ge(pair_slots_ready, 1)
            for t in range(T):
                for k in range(2):
                    pool.indirect_dma_start(
                        out=token_table, out_offset=bass.IndirectOffsetOnAxis(ap=pair_slot[:, k, t:t + 1], axis=0),
                        in_=norm[:, t, :], in_offset=None).then_inc(tokens_out, 16)

            pool.wait_ge(y_stored[0], 16 * (NBLK // 2))
            pool.wait_ge(y_stored[1], 16 * (NBLK // 2))
            for t in range(T):
                if t >= RING:
                    pool.wait_ge(rows_added, t - RING + 1)
                for k in range(2):
                    pool.indirect_dma_start(
                        out=y_ring[:, 2 * (t % RING) + k, :], out_offset=None, in_=expert_out,
                        in_offset=bass.IndirectOffsetOnAxis(ap=pair_slot[:, k, t:t + 1], axis=0))\
                        .then_inc(rows_back[t % RING], 16)

        @block.scalar
        def _(act):
            steps = Steps(act, s_act)

            def copy(out, in_):
                return act.copy(out, in_)

            act.wait_ge(s_edges, 48)
            rec3 = rec.rearrange("p (c r) -> p c r", r=3)
            copy(rec3[:, :, 0], dst_i)
            copy(rec3[:, :, 2], wgt).then_inc(slots_ready, 1)

            act.sem_inc(proj_free_act, 1)
            act.wait_ge(var_ready, 1)
            act.activation(rstd, rstd, ACT.Sqrt).then_inc(std_ready, 1)
            with act.Fori(0, T) as t:
                act.wait_ge(xnT_psum, t + 1)
                copy(xnT, ps[:, 0, 0:DC * P].rearrange("p (c n) -> p c n", c=DC)).then_inc(xnT_ready, 1)
                act.wait_ge(proj_ready, t + 1)
                copy(normf[:, bass.ds(t * D, D)], ps[0:P, 1, 0:D]).then_inc(support_ready, 1)
                copy(V[:, bass.ds(t * D, D)], ps[0:P, 1, D:2 * D]).then_inc(proj_free_act, 1)
                act.wait_ge(q_shifted, t + 1)
                act.activation(Q[:, bass.ds(t * D, D)], Q[:, bass.ds(t * D, D)], ACT.Exp).then_inc(q_exped, 1)
            act.wait_ge(kshift_psum, 1)
            copy(kshift, ps[0:P, 1, 0:D]).then_inc(kshift_ready, 1)
            with act.Fori(0, T) as t:
                act.wait_ge(k_shifted, t + 1)
                act.activation(K[:, bass.ds(t * D, D)], K[:, bass.ds(t * D, D)], ACT.Exp).then_inc(k_exped, 1)
            act.wait_ge(q_ready, T)
            with act.Fori(0, T) as t:
                copy(xn, Q[:, bass.ds(t * D, D)]).then_inc(q_staged, 1)
                act.wait_ge(qT_psum, t + 1)
                copy(qT, ps[:, 0, 0:DC * P].rearrange("p (c n) -> p c n", c=DC)).then_inc(qT_ready, 1)
                act.wait_ge(mix_psum, t + 1)
                copy(K[:, bass.ds(t * D, D)], ps[0:P, 1, 0:D]).then_inc(mix_copied, 1)
            act.wait_ge(var_ready, 2)
            act.activation(rstd, rstd, ACT.Sqrt).then_inc(std_ready, 1)

            act.wait_ge(var_ready, 3)
            act.activation(rstd, rstd, ACT.Sqrt).then_inc(std_ready, 1)

            def router_copy(t, k):
                act.wait_ge(norm_ready, t + 1)
                copy(normf[:, bass.ds(t * D, D)], rxn[:, k, :])
                act.wait_ge(rT_psum, t + 1)
                copy(rxT[:, k, :, :], ps[:, 4 + k, 0:DC * P].rearrange("p (c n) -> p c n", c=DC)).then_inc(rT_ready, 1)

            with act.Fori(0, T // 2) as i:
                router_copy(2 * i, 0)
                router_copy(2 * i + 1, 1)
            router_copy(T - 1, 0)
            act.wait_ge(var_ready, 4)
            act.activation(probs, probs, ACT.Exp).then_inc(std_ready, 1)

            def xt_copy(j):
                act.wait_ge(xt_psum, j + 1)
                copy(XT, ps[:, 4, 0:DC * L].rearrange("p (c n) -> p c n", c=DC)).then_inc(xt_ready, 1)

            def do_silu(j):
                act.wait_ge(h_ready, j + 1)
                act.activation(silu, ps[:, 0:2, 0:HB], ACT.Silu).then_inc(silu_ready, 1)

            def gt_copy(j):
                act.wait_ge(gT_psum, j + 1)
                copy(GT[:, 0:4, :], ps[:, 5, :].rearrange("p (c n) -> p c n", n=L)).then_inc(gT_act, 1)

            xt_copy(0)
            do_silu(0)
            xt_copy(1)
            with act.Fori(1, NBLK - 1) as j:
                do_silu(j)
                gt_copy(j - 1)
                xt_copy(j + 1)
            do_silu(NBLK - 1)
            gt_copy(NBLK - 2)
            gt_copy(NBLK - 1)

        @block.tensor
        def _(pe):
            pe.wait_ge(s_const, 8)
            pe.wait_ge(count_ready, 1)
            pe.matmul(ps[0:P, 3, 0:T], upper[:], count, start=True, stop=True)
            pe.matmul(ps[:, 3, 32:32 + T], ones[:], count, start=True, stop=True).then_inc(base_ready, 1)

            pe.sem_inc(xn_free, 1)
            pe.wait_ge(s_w, 16 * 6)
            with pe.Fori(0, T) as t:
                pe.wait_ge(xn_ready, t + 1)
                for c in range(DC):
                    mm = pe.transpose(ps[:, 0, c * P:(c + 1) * P], xn[:, c * L:(c + 1) * L], ident[0:P, 0:P])
                mm.then_inc(xnT_psum, 1)
                pe.sem_inc(xn_free, 1)
                pe.wait_ge(xnT_ready, t + 1)
                pe.wait_ge(proj_free_act, t + 1)
                pe.wait_ge(proj_free_dve, t + 1)
                for n in range(2):
                    for c in range(DC):
                        mm = pe.matmul(ps[0:P, 1 + n, :], xnT[:, c, :], wqkvg[:, c, n * 512:(n + 1) * 512],
                                       start=(c == 0), stop=(c == DC - 1))
                mm.then_inc(proj_ready, 1)
            pe.wait_ge(kmaxT_ready, 1)
            for c in range(DC):
                mm = pe.transpose(ps[:, 0, c * P:(c + 1) * P], kmax[:, c * L:(c + 1) * L], ident[0:P, 0:P])
            mm.then_inc(kmaxT_ready, 1)
            pe.wait_ge(kmaxb_ready, 1)
            for c in range(DC):
                mm = pe.matmul(ps[0:P, 1, c * L:(c + 1) * L], kmaxb[:, c, :], ident[:], start=True, stop=True)
            mm.then_inc(kshift_psum, 1)

            def context(t, start, stop):
                pe.wait_ge(k_exped, t + 1)
                for c in range(DC):
                    kk = K[:, bass.ds(t * D + c * L, L)]
                    pe.matmul(ps[:, 4 + c, 0:L], V[:, bass.ds(t * D + c * L, L)], kk, start=start, stop=stop)
                    mm = pe.matmul(ps[:, 6 + c, 0:1], kk, ones[:, 0:1], start=start, stop=stop)
                return mm

            for t in range(T):
                mm = context(t, t == 0, t == T - 1)
            mm.then_inc(ctx_ready, 1)
            pe.wait_ge(ctxT_ready, 1)
            for c in range(DC):
                mm = pe.matmul(ps[:, 1, c * D:(c + 1) * D], ctxT[:, c, :], wout_sb[:, c, :], start=True, stop=True)
            mm.then_inc(mixw_psum, 1)
            pe.wait_ge(mixw_ready, 1)
            with pe.Fori(0, T) as t:
                pe.wait_ge(q_staged, t + 1)
                for c in range(DC):
                    mm = pe.transpose(ps[:, 0, c * P:(c + 1) * P], xn[:, c * L:(c + 1) * L], ident[0:P, 0:P])
                mm.then_inc(qT_psum, 1)
                pe.wait_ge(qT_ready, t + 1)
                for c in range(DC):
                    mm = pe.matmul(ps[0:P, 1, 0:D], qT[:, c, :], mix_w[:, c, :], start=(c == 0), stop=(c == DC - 1))
                mm.then_inc(mix_psum, 1)

            for k in range(GU):
                pe.sem_inc(chunk_summed, 1)
            with pe.Fori(0, GTURNS) as i:
                for k in range(GU):
                    pe.wait_ge(onehot_ready, i * GU + k + 1)
                    pe.wait_ge(gathered[k], 16 * (i + 1))
                    pe.wait_ge(chunk_added, i * GU + k + 1)
                    pe.matmul(ps[0:P, k % QK, 0:D], onehot[:, k, :], gbuf[:, k, :], start=True, stop=True)\
                        .then_inc(chunk_summed, 1)

            def router(t, k):
                pe.wait_ge(norm_ready, t + 1)
                for c in range(DC):
                    mm = pe.transpose(ps[:, 4 + k, c * P:(c + 1) * P], rxn[:, k, c * L:(c + 1) * L], ident[0:P, 0:P])
                mm.then_inc(rT_psum, 1)
                pe.wait_ge(rT_ready, t + 1)
                for c in range(DC):
                    mm = pe.matmul(ps[0:P, 6, bass.ds(t * XP, XP)], rxT[:, k, c, :], wr_sb[:, c, :],
                                   start=(c == 0), stop=(c == DC - 1))
                mm.then_inc(logits_ready, 1)

            with pe.Fori(0, T // 2) as i:
                router(2 * i, 0)
                router(2 * i + 1, 1)
            router(T - 1, 0)
            pe.wait_ge(pair_count_ready, 1)
            pe.matmul(ps[0:P, 7, 0:XP], upper[:], count[:, 0:XP], start=True, stop=True)
            pe.matmul(ps[:, 7, 32:32 + XP], ones[:], count[:, 0:XP], start=True, stop=True).then_inc(pair_base_ready, 1)

            pe.wait_ge(expert_map_ready, 1)
            pe.wait_ge(s_wup, 16 * 2 * XP)

            def expert(j):
                return pe.value_load(block_expert[0:1, bass.ds(j, 1)], min_val=0, max_val=XP - 1)

            def x_transpose(j, k, turn):
                pe.wait_ge(x_loaded[k], 16 * turn)
                for c in range(DC):
                    mm = pe.transpose(ps[:, 4, c * L:(c + 1) * L], X[k][:, c * L:(c + 1) * L], ident[:])
                mm.then_inc(xt_psum, 1)

            def up(j, e):
                pe.wait_ge(xt_ready, j + 1)
                for n in range(4):
                    for c in range(DC):
                        mm = pe.matmul(ps[:, n, 0:HB], XT[:, c, :],
                                       wup[:, bass.ds(e * (DC * 2 * H) + (c * 2 * H + n * HB), HB)],
                                       start=(c == 0), stop=(c == DC - 1))
                mm.then_inc(h_ready, 1)

            def g_transpose(j, k):
                pe.wait_ge(g_ready, j + 1)
                for c in range(HC):
                    w = L if c < HC - 1 else HL
                    mm = pe.transpose(ps[0:w, 5 + c // 4, (c % 4) * L:(c % 4 + 1) * L], G[k][:, c * L:c * L + w], ident[:])
                mm.then_inc(gT_psum, 1)

            def down(j, e):
                pe.wait_ge(gT_act, j + 1)
                pe.wait_ge(gT_dve, j + 1)
                for c in range(HC):
                    w = L if c < HC - 1 else HL
                    mm = pe.matmul(ps[:, 7, 0:D], GT[0:w, c, :], wdn[0:w, bass.ds(e * (HC * D) + c * D, D)],
                                   start=(c == 0), stop=(c == HC - 1))
                mm.then_inc(y_psum, 1)

            x_transpose(0, 0, 1)
            up(0, expert(0))
            x_transpose(1, 1, 1)

            def turn(j, k, loads, more):
                e, before = expert(j), expert(j - 1)
                pe.wait_ge(g_ready, j)
                up(j, e)
                g_transpose(j - 1, 1 - k)
                if more:
                    x_transpose(j + 1, 1 - k, loads)
                if not isinstance(j, int) or j >= 2:
                    pe.wait_ge(y_ready, j - 1)
                down(j - 1, before)

            turn(1, 1, 2, True)
            turn(2, 0, 2, True)
            with pe.Fori(1, NBLK // 2 - 1) as i:
                turn(2 * i + 1, 1, i + 2, True)
                turn(2 * i + 2, 0, i + 2, True)
            turn(NBLK - 1, 1, 0, False)
            g_transpose(NBLK - 1, 1)
            pe.wait_ge(y_ready, NBLK - 1)
            down(NBLK - 1, expert(NBLK - 1))

        @block.vector
        def _(dve):
            v = nc.vector
            steps = Steps(dve, s_dve)
            v.memset(rank, 0.0).then_inc(s_dve, 1)
            v.memset(kmax, -3.0e38).then_inc(s_dve, 1)
            v.memset(ctxT, 0.0).then_inc(s_dve, 1)
            steps.n = 3
            dve.sem_inc(proj_free_dve, 1)
            for k in range(QK):
                dve.sem_inc(chunk_added, 1)

            dve.wait_ge(s_edges, 48)
            dve.wait_ge(s_const, 8)
            steps.link(v.tensor_scalar(tmp, src_i, 1.0 / T, -0.5 + 0.5 / T, ALU.mult, ALU.add))
            steps.link(v.tensor_scalar(row_of, tmp, ROUND, -ROUND, ALU.add, ALU.add))
            steps.link(v.scalar_tensor_tensor(tile_of, row_of, -float(T), src_i, ALU.mult, ALU.add))
            v.tensor_copy(rec.rearrange("p (c r) -> p c r", r=3)[:, :, 1], row_of).then_inc(s_dve, 1)
            steps.n += 1
            with steps.loop(0, T, 1) as b:
                steps.mark(v.tensor_scalar(tmp, tile_of, tile_no[0:P, bass.ds(b, 1)], 0.0, ALU.is_equal, ALU.add,
                                           accum_out=count[:, bass.ds(b, 1)]))
                steps.wait()
            v.engine_nop().then_inc(count_ready, 1)

            def block_counts(nb, bank):
                steps.link(v.tensor_scalar(blocks[:, 0:nb], ps[:, bank, 32:32 + nb], 1.0 / L, 0.5 - 0.5 / L,
                                           ALU.mult, ALU.add))
                steps.link(v.tensor_scalar(blocks[:, 0:nb], blocks[:, 0:nb], ROUND, -ROUND, ALU.add, ALU.add))
                steps.link(v.tensor_tensor_scan(blocks_to[:, 0:nb], blocks[:, 0:nb], blocks[:, 0:nb], 0.0,
                                                ALU.add, ALU.max))
                steps.link(v.tensor_tensor(first_slot[:, 0:nb], blocks_to[0:P, 0:nb], blocks[0:P, 0:nb], ALU.subtract))
                steps.link(v.scalar_tensor_tensor(first_slot[:, 0:nb], first_slot[:, 0:nb], float(L),
                                                  ps[0:P, bank, 0:nb], ALU.mult, ALU.add))

            dve.wait_ge(base_ready, 1)
            block_counts(T, 3)
            cumul = ps[0:P, 7, 0:C]
            with steps.loop(0, T, 3) as b:
                steps.link(v.tensor_scalar(mask, tile_of, tile_no[0:P, bass.ds(b, 1)], None, ALU.is_equal))
                steps.link_apart(v.tensor_tensor_scan(cumul, mask, mask, first_slot[:, bass.ds(b, 1)], ALU.add, ALU.max))
                steps.link(v.copy_predicated(rank, mask, cumul))
            steps.link(v.tensor_scalar(rank, rank, -1.0, None, ALU.add))
            steps.link(v.tensor_scalar(tmp, rank, 1.0 / L, -0.5 + 0.5 / L, ALU.mult, ALU.add))
            steps.link(v.tensor_scalar(tmp, tmp, ROUND, -ROUND, ALU.add, ALU.add))
            steps.link(v.scalar_tensor_tensor(tmp2, tmp, -float(L), rank, ALU.mult, ALU.add))
            v.scalar_tensor_tensor(slot_i, tmp2, float(NCH), tmp, ALU.mult, ALU.add).then_inc(slots_ready, 1)

            dve.wait_ge(s_x, 16)
            dve.wait_ge(s_x2, 16)

            def tile_stats(t):
                return stats6[:, bass.ds(t * 6, 6)]

            def deviation(turn):
                steps.mark(v.tensor_tensor(mean, stats[:, :, 1], stats[:, :, 4], ALU.add))
                steps.mark(v.tensor_tensor(spread, stats[:, :, 1], stats[:, :, 4], ALU.subtract))
                steps.link(v.tensor_tensor(rstd, stats[:, :, 2], stats[:, :, 5], ALU.add))
                steps.mark(v.tensor_scalar(mean, mean, 0.5, None, ALU.mult))
                steps.mark(v.tensor_tensor(spread, spread, spread, ALU.mult))
                steps.link(v.tensor_scalar(rstd, rstd, 1.0 / D, EPS, ALU.mult, ALU.add))
                v.scalar_tensor_tensor(rstd, spread, 0.25, rstd, ALU.mult, ALU.add).then_inc(var_ready, 1)
                dve.wait_ge(std_ready, turn)
                steps.link(v.reciprocal(rstd, rstd))

            def acc_tile(t):
                return accf[:, bass.ds(t * D, D)]

            with steps.loop(0, T, 1) as t:
                steps.link(v.bn_stats(tile_stats(t), acc_tile(t)))
            deviation(1)

            with steps.loop(0, T, 6) as t:
                dve.wait_ge(xn_free, t + 1)
                v.tensor_scalar(xn, acc_tile(t), mean[:, bass.ds(t, 1)], rstd[:, bass.ds(t, 1)],
                                ALU.subtract, ALU.mult).then_inc(xn_ready, 1)
                dve.wait_ge(proj_ready, t + 1)
                qt = Q[:, bass.ds(t * D, D)].rearrange("p (h d) -> p h d", h=HEADS)
                steps.link(v.tensor_reduce(qmax, ps[0:P, 2, 0:D].rearrange("p (h d) -> p h d", h=HEADS),
                                           AX.X, ALU.max))
                v.tensor_tensor(qt, ps[0:P, 2, 0:D].rearrange("p (h d) -> p h d", h=HEADS),
                                qmax.unsqueeze(2).broadcast_to([P, HEADS, DH]), ALU.subtract).then_inc(q_shifted, 1)
                steps.mark(v.tensor_copy(K[:, bass.ds(t * D, D)], ps[0:P, 2, D:2 * D]))
                steps.link(v.tensor_tensor(kmax, ps[0:P, 2, D:2 * D], kmax, ALU.max))
                dve.sem_inc(proj_free_dve, 1)
                dve.wait_ge(q_exped, t + 1)
                apart(dve)
                steps.link(v.tensor_reduce(qsum, qt, AX.X, ALU.add))
                steps.link(v.reciprocal(qrec, qsum))
                v.tensor_tensor(qt, qt, qrec.unsqueeze(2).broadcast_to([P, HEADS, DH]), ALU.mult).then_inc(q_ready, 1)
                steps.link(v.engine_nop())
            v.engine_nop().then_inc(kmaxT_ready, 1)

            dve.wait_ge(kmaxT_ready, 2)
            steps.link(v.tensor_reduce(kneg, ps[:, 0, 0:DC * P].rearrange("p (c n) -> p c n", c=DC), AX.X, ALU.max))
            v.tensor_copy(kmaxb, kneg.unsqueeze(2).broadcast_to([L, DC, P])).then_inc(kmaxb_ready, 1)
            dve.wait_ge(kshift_ready, 1)
            with dve.Fori(0, T) as t:
                kt = K[:, bass.ds(t * D, D)]
                v.tensor_tensor(kt, kt, kshift, ALU.subtract).then_inc(k_shifted, 1)

            dve.wait_ge(ctx_ready, 1)
            for c in range(DC):
                for h in range(HPC):
                    r = slice(h * DH, (h + 1) * DH)
                    steps.mark(v.tensor_copy(ctxT[r, c, r], ps[r, 4 + c, r]))
            v.engine_nop().then_inc(ctxT_ready, 1)
            for c in range(DC):
                steps.link(v.reciprocal(krec[:, c:c + 1], ps[:, 6 + c, 0:1]))
            steps.link(v.tensor_scalar(krec, krec, SCALE, None, ALU.mult))
            dve.wait_ge(mixw_psum, 1)
            for c in range(DC):
                steps.mark(v.tensor_scalar(mix_w[:, c, :], ps[:, 1, c * D:(c + 1) * D], krec[:, c:c + 1], None, ALU.mult))
            steps.wait()
            v.engine_nop().then_inc(mixw_ready, 1)

            with steps.loop(0, T, 1) as t:
                dve.wait_ge(mix_copied, t + 1)
                steps.link(v.bn_stats(tile_stats(t), K[:, bass.ds(t * D, D)]))
            deviation(2)
            with steps.loop(0, T, 3) as t:
                qt = K[:, bass.ds(t * D, D)]
                steps.link(v.tensor_scalar(qt, qt, mean[:, bass.ds(t, 1)], rstd[:, bass.ds(t, 1)],
                                           ALU.subtract, ALU.mult))
                steps.link(v.tensor_tensor(qt, qt, gamma_sb, ALU.mult))
                steps.link(v.tensor_tensor(acc_tile(t), acc_tile(t), qt, ALU.add))

            def bucket_map(out_i, number, total, nb):
                steps.link(v.memset(total, 0.0))
                for b in range(nb - 1):
                    steps.link(v.scalar_tensor_tensor(total, number, blocks_to[0:1, b:b + 1], total,
                                                      ALU.is_ge, ALU.add))
                return v.tensor_copy(out_i, total)

            steps.link(bucket_map(chunk_tile[:], chunk_no, chunk_acc, T))
            v.engine_nop().then_inc(arena_free, 1)

            dve.wait_ge(s_recs, 16)
            dve.wait_ge(s_support_out, 32)
            rin = rec_in.rearrange("p (c r) -> p c r", r=3)
            steps.link(v.tensor_copy(gidx, rin[:, :, 0]))
            v.engine_nop().then_inc(gidx_ready, 1)
            with steps.loop(0, GTURNS, 0) as i:
                tiles = [dve.value_load(chunk_tile[0:1, bass.ds(i * GU + k, 1)], min_val=0, max_val=T - 1)
                         for k in range(GU)]
                for k in range(GU):
                    base = (i * GU + k) * 3
                    v.tensor_scalar(onehot[:, k, :], lane_no[:], rec_in[:, bass.ds(base + 1, 1)],
                                    rec_in[:, bass.ds(base + 2, 1)], ALU.is_equal, ALU.mult).then_inc(onehot_ready, 1)
                for k in range(GU):
                    dve.wait_ge(chunk_summed, GU + i * GU + k + 1)
                    a = accf[:, bass.ds(tiles[k] * D, D)]
                    v.tensor_tensor(a, a, ps[0:P, k % QK, 0:D], ALU.add).then_inc(chunk_added, 1)
                    dve.wait_ge(chunk_added, QK + i * GU + k + 1)

            with steps.loop(0, T, 1) as t:
                steps.link(v.bn_stats(tile_stats(t), acc_tile(t)))
            deviation(3)

            def norm_tile(t, k, first):
                if not first:
                    dve.wait_ge(rT_ready, t - 1)
                v.tensor_scalar(rxn[:, k, :], acc_tile(t), mean[:, bass.ds(t, 1)],
                                rstd[:, bass.ds(t, 1)], ALU.subtract, ALU.mult).then_inc(norm_ready, 1)

            norm_tile(0, 0, True)
            norm_tile(1, 1, True)
            with dve.Fori(1, T // 2) as i:
                norm_tile(2 * i, 0, False)
                norm_tile(2 * i + 1, 1, False)
            norm_tile(T - 1, 0, False)
            dve.wait_ge(logits_ready, T)
            lg = ps[0:P, 6, 0:TX].rearrange("p (t e) -> p t e", e=XP)

            def over_experts(a):
                return a.unsqueeze(2).broadcast_to([P, T, XP])

            def over_tiles(a):
                return a.unsqueeze(1).broadcast_to([P, T, XP])

            steps.link(v.tensor_reduce(r1[0], lg, AX.X, ALU.max))
            v.tensor_tensor(probs, lg, over_experts(r1[0]), ALU.subtract).then_inc(var_ready, 1)
            dve.wait_ge(std_ready, 4)
            steps.link(v.tensor_reduce(r1[0], probs, AX.X, ALU.add))
            steps.link(v.reciprocal(r1[1], r1[0]))
            steps.link(v.tensor_tensor(probs, probs, over_experts(r1[1]), ALU.mult))

            def pick(mine, top):
                steps.link(v.tensor_reduce(top, probs, AX.X, ALU.max))
                steps.link(v.tensor_tensor(key, probs, over_experts(top), ALU.is_equal))
                steps.link(v.tensor_tensor(key, key, over_tiles(expert_rev[:]), ALU.mult))
                steps.link(v.tensor_reduce(r1[0], key, AX.X, ALU.max))
                steps.link(v.tensor_tensor(mine, key, over_experts(r1[0]), ALU.is_equal))

            pick(first, r1[1])
            steps.link(v.scalar_tensor_tensor(probs, first, -2.0, probs, ALU.mult, ALU.add))
            pick(second, r1[2])
            steps.link(v.tensor_tensor(r1[0], r1[1], r1[2], ALU.add))
            steps.link(v.tensor_scalar(r1[0], r1[0], 1e-9, None, ALU.add))
            steps.link(v.reciprocal(r1[3], r1[0]))
            steps.mark(v.tensor_tensor(gate[:, 0, :], r1[1], r1[3], ALU.mult))
            steps.mark(v.tensor_tensor(gate[:, 1, :], r1[2], r1[3], ALU.mult))
            steps.link(v.tensor_tensor(both, first, second, ALU.add))
            for e in range(XP):
                steps.mark(v.tensor_tensor_scan(cum[:, :, e], both[:, :, e], both[:, :, e], 0.0, ALU.add, ALU.max))
            steps.wait()
            v.tensor_copy(count[:, 0:XP], cum[:, T - 1, :]).then_inc(pair_count_ready, 1)
            dve.wait_ge(pair_base_ready, 1)
            block_counts(XP, 7)
            steps.link(v.tensor_scalar(first_slot[:, 0:XP], first_slot[:, 0:XP], -1.0, None, ALU.add))
            steps.link(v.tensor_tensor(place, cum, over_tiles(first_slot[:, 0:XP]), ALU.add))
            for k, mine in enumerate((first, second)):
                steps.link(v.tensor_tensor(key, mine, place, ALU.mult))
                steps.link(v.tensor_reduce(r1[k], key, AX.X, ALU.add))
                steps.link(v.tensor_copy(pair_slot[:, k, :], r1[k]))
            v.engine_nop().then_inc(pair_slots_ready, 1)
            steps.link(bucket_map(block_expert[:], block_no, block_acc, XP))
            v.engine_nop().then_inc(expert_map_ready, 1)

            def gated(j, k):
                dve.wait_ge(silu_ready, j + 1)
                v.tensor_tensor(G[k].rearrange("p (a n) -> p a n", a=2), ps[:, 2:4, 0:HB], silu, ALU.mult)\
                 .then_inc(g_ready, 1)

            def gt_copy(j):
                dve.wait_ge(gT_psum, j + 1)
                v.tensor_copy(GT[:, 4, :], ps[:, 6, 0:L])
                v.tensor_copy(GT[0:HL, 5, :], ps[0:HL, 6, L:2 * L]).then_inc(gT_dve, 1)

            def y_copy(j, k, stored):
                dve.wait_ge(y_psum, j + 1)
                if stored is not None:
                    dve.wait_ge(y_stored[k], 16 * stored)
                v.tensor_copy(Y[k], ps[:, 7, 0:D]).then_inc(y_ready, 1)

            def turn(j, k, stored):
                dve.wait_ge(gT_psum, j - 1) if not isinstance(j, int) or j >= 2 else None
                gated(j, k)
                gt_copy(j - 1)
                y_copy(j - 1, 1 - k, stored)

            dve.wait_ge(tokens_out, 16 * 2 * T)
            gated(0, 0)
            turn(1, 1, None)
            turn(2, 0, None)
            with dve.Fori(1, NBLK // 2 - 1) as i:
                turn(2 * i + 1, 1, i)
                turn(2 * i + 2, 0, i)
            turn(NBLK - 1, 1, NBLK // 2 - 1)
            gt_copy(NBLK - 1)
            y_copy(NBLK - 1, 1, NBLK // 2 - 1)

            with steps.loop(0, T // RING, RING) as i:
                for r in range(RING):
                    t = i * RING + r
                    dve.wait_ge(rows_back[r], 32 * (i + 1))
                    steps.link(v.scalar_tensor_tensor(acc_tile(t), y_ring[:, 2 * r, :], gate[:, 0, bass.ds(t, 1)],
                                                      acc_tile(t), ALU.mult, ALU.add))
                    v.scalar_tensor_tensor(acc_tile(t), y_ring[:, 2 * r + 1, :], gate[:, 1, bass.ds(t, 1)],
                                           acc_tile(t), ALU.mult, ALU.add).then_inc(rows_added, 1)


def kernel(x, src, dst, edge_weight, L0_gnn_W, L0_mix_Wqkv, L0_mix_Wout, L0_mix_gamma,
           L0_ffn_router_w, L0_ffn_w1, L0_ffn_w2, L0_ffn_w3):
    import numpy as np
    import concourse.bacc as _bacc
    from concourse import mybir as _mybir
    from concourse.bass_utils import run_bass_kernel_spmd as _run

    L = 128
    N, D = x.shape
    E = src.shape[0]
    XP, H, _ = L0_ffn_w1.shape
    HC = -(-H // L)
    T = 25
    w1, w2, w3 = (np.asarray(a) for a in (L0_ffn_w1, L0_ffn_w2, L0_ffn_w3))
    w_up = np.concatenate([w1, w3], axis=1).transpose(2, 0, 1).reshape(D // L, L, XP, 2 * H).transpose(1, 2, 0, 3)
    w_down = np.zeros((XP, HC * L, D), w2.dtype)
    w_down[:, :H, :] = w2.transpose(0, 2, 1)
    w_down = w_down.reshape(XP, HC, L, D).transpose(2, 0, 1, 3)
    ins = {
        "x": np.asarray(x), "src": np.asarray(src), "dst": np.asarray(dst), "edge_weight": np.asarray(edge_weight),
        "w_gnn": np.asarray(L0_gnn_W), "w_qkv": np.asarray(L0_mix_Wqkv), "w_out": np.asarray(L0_mix_Wout),
        "gamma": np.broadcast_to(np.asarray(L0_mix_gamma), (N // T, D)), "w_router": np.asarray(L0_ffn_router_w).T,
        "w_up": w_up, "w_down": w_down,
    }
    nc = _bacc.Bacc("TRN2", target_bir_lowering=False, num_devices=1)
    f32 = _mybir.dt.float32
    arrays, args = {}, []
    for name, a in ins.items():
        a = np.ascontiguousarray(a)
        arrays[f"in_{name}"] = a
        args.append(nc.dram_tensor(f"in_{name}", a.shape, _mybir.dt.from_np(a.dtype), kind="ExternalInput").ap())
    args.append(nc.dram_tensor("x_out", (N, D), f32, kind="ExternalOutput").ap())
    chunks = -(-((E + T * (L - 1)) // L) // 8) * 8
    blocks = (2 * N + XP * (L - 1)) // L
    args.append(nc.dram_tensor("support_table", (N, D), f32, kind="Internal").ap())
    args.append(nc.dram_tensor("edge_table", (L * chunks, 3), f32, kind="Internal").ap())
    args.append(nc.dram_tensor("token_table", (blocks * L, D), f32, kind="Internal").ap())
    args.append(nc.dram_tensor("expert_out", (blocks * L, D), f32, kind="Internal").ap())
    gps_layer_program(nc, *args)
    r = _run(nc, [arrays], core_ids=[0])
    return r.results[0]["x_out"]
```

```python
import concourse.bass as bass
from concourse import mybir
from contextlib import ExitStack, contextmanager


def gps_layer_program(nc, x, src, dst, edge_weight, w_gnn, w_qkv, w_out, gamma, w_router, w_up, w_down,
                      x_out, support_table, edge_table, norm_table):
    f32, i32, u8 = mybir.dt.float32, mybir.dt.int32, mybir.dt.uint8
    ALU, ACT, AX = mybir.AluOpType, mybir.ActivationFunctionType, mybir.AxisListType

    L = 128
    N, D = x.shape
    T = 25
    P = N // T
    E = src.shape[0]
    C = E // P
    DC = D // L
    HEADS, DH = 8, 32
    HPC = L // DH
    XP = w_router.shape[1]
    H = w_up.shape[3] // 2
    HB = H // 2
    HC = -(-H // L)
    HL = H - (HC - 1) * L
    EPS = 1e-05
    SCALE = DH ** -0.5
    ROUND = 1.5 * 2.0 ** 23

    GU = 8
    GTURNS = -(-((E + T * (L - 1)) // L) // GU)
    NCH = GTURNS * GU
    NBLK = (2 * N + XP * (L - 1)) // L
    SA, SB_ = 9, 8
    SU = SA + SB_
    STURNS = C // SU
    QK = 4
    GB = 5
    assert STURNS * SU == C and P * T == N and P * C == E and T % GB == 0 and T % 2 and NBLK % 2 == 0

    ctx = ExitStack()
    with ctx:
        def sb(name, shape, dt=f32):
            return ctx.enter_context(nc.sbuf_tensor(name, shape, dt))

        def sem(name):
            return ctx.enter_context(nc.semaphore(name))

        acc = sb("acc", [P, T, D])
        norm_all = sb("norm", [L, T * D])
        norm = norm_all[0:P, :].rearrange("p (t d) -> p t d", d=D)
        gbuf = norm_all[:, 0:GU * D].rearrange("p (k n) -> p k n", k=GU)
        onehot = norm_all[:, GU * D:GU * (D + P)].rearrange("p (k n) -> p k n", k=GU)
        accf = acc[:, :, :].rearrange("p t d -> p (t d)")
        normf = norm_all[0:P, :]
        ident = sb("ident", [L, L])
        upper = sb("upper", [P, P])
        ones = sb("ones", [P, L])
        lane_row = sb("lane_row", [L, L])
        lane_no = lane_row[:, 0:P]
        chunk_tile = sb("chunk_tile", [1, NCH], i32)
        block_expert = sb("block_expert", [1, NBLK], i32)
        small = sb("small", [L, 960])

        WUP, WDN = XP * DC * 2 * H, XP * HC * D
        arena = sb("arena", [L, WUP + WDN])
        wup = arena[:, 0:WUP]
        wdn = arena[:, WUP:WUP + WDN]
        at = [0]

        def carve(cols, rows=L):
            a = at[0]
            at[0] += cols
            assert at[0] <= WUP + WDN
            return arena[0:rows, a:a + cols]

        src_i, dst_i = carve(C, P).bitcast(i32), carve(C, P).bitcast(i32)
        wgt = carve(C, P)
        tile_of = carve(C, P)
        row_of = carve(C, P)
        rank = carve(C, P)
        tmp = carve(C, P)
        tmp2 = carve(C, P)
        mask = [carve(C // 4 + 1, P).bitcast(u8)[:, 0:C] for _ in range(GB)]
        zeros = carve(NCH * 3)
        chunk_no = carve(NCH, 1)
        chunk_acc = carve(NCH, 1)
        wqkvg = carve(DC * 4 * D).rearrange("p (c n) -> p c n", c=DC)
        wout_sb = carve(DC * D).rearrange("p (c n) -> p c n", c=DC)
        gamma_sb = carve(D, P)
        row_in = [carve(D, P), carve(D, P)]
        row_T = [carve(DC * P).rearrange("p (c n) -> p c n", c=DC) for _ in range(2)]
        Q = carve(T * D, P)
        K = carve(T * D, P)
        V = carve(T * D, P)
        kmax = carve(D, P)
        kshift = carve(D, P)
        kmaxb = carve(DC * P).rearrange("p (c n) -> p c n", c=DC)
        ctxT = carve(DC * L).rearrange("p (c n) -> p c n", c=DC)
        mix_w = carve(DC * D).rearrange("p (c n) -> p c n", c=DC)
        WORK = 2 * D + DC * L + 3 * H + HC * L + 2 * D
        work = sb("work", [L, WORK])
        rec_in = work[:, 0:NCH * 3]
        gidx = work[:, NCH * 3:NCH * 4].bitcast(i32)
        rec = work[0:P, NCH * 4:NCH * 4 + 3 * C]
        slot_i = work[0:P, NCH * 4 + 3 * C:NCH * 4 + 4 * C].bitcast(i32)
        wat = [0]

        def wcarve(cols):
            a = wat[0]
            wat[0] += cols
            assert wat[0] <= WORK
            return work[:, a:a + cols]

        X = [wcarve(D), wcarve(D)]
        XT = wcarve(DC * L).rearrange("p (c n) -> p c n", c=DC)
        silu = wcarve(H).rearrange("p (a n) -> p a n", a=2)
        G = [wcarve(H), wcarve(H)]
        GT = wcarve(HC * L).rearrange("p (c n) -> p c n", c=HC)
        Y = [wcarve(D), wcarve(D)]

        stage_slot = [sb("stage_slot0", [P, SA], i32), sb("stage_slot1", [P, SB_], i32)]
        stage_rec = [sb("stage_rec0", [P, SA * 3]), sb("stage_rec1", [P, SB_ * 3])]
        stage_gidx = [sb("stage_gidx0", [L, GU // 2], i32), sb("stage_gidx1", [L, GU // 2], i32)]
        stage_token = [sb("stage_token0", [L, 1], i32), sb("stage_token1", [L, 1], i32)]
        stage_dest = [sb("stage_dest0", [L, 1], i32), sb("stage_dest1", [L, 1], i32)]

        so = [0]

        def s_carve(cols, rows=L):
            a = so[0]
            so[0] += cols
            assert so[0] <= 960
            return small[0:rows, a:a + cols]

        tile_no = s_carve(T)
        count = s_carve(T, P)
        first_slot = s_carve(T, P)
        blocks = s_carve(T)
        blocks_to = s_carve(T)
        stats6 = s_carve(6 * T, P)
        stats = stats6.rearrange("p (t s) -> p t s", s=6)
        mean = s_carve(T, P)
        spread = s_carve(T, P)
        rstd = s_carve(T, P)
        qmax = s_carve(HEADS, P)
        qsum = s_carve(HEADS, P)
        qrec = s_carve(HEADS, P)
        kneg = s_carve(DC)
        krec = s_carve(DC)
        wr_sb = s_carve(DC * XP).rearrange("p (c n) -> p c n", c=DC)
        gate = s_carve(2 * T, P).rearrange("p (k t) -> p k t", k=2)
        node_no = s_carve(T, P)
        lane = s_carve(1)
        block_no = s_carve(NBLK, P)
        block_acc = s_carve(NBLK, 1)
        block_token = s_carve(NBLK).bitcast(i32)
        block_dest = s_carve(NBLK).bitcast(i32)
        block_gate = s_carve(NBLK)
        block_node = s_carve(NBLK)
        block_empty = s_carve(NBLK)

        TX = T * XP
        rw = work[0:P, 0:7 * TX + 4 * T]

        def r3(n):
            return rw[:, n * TX:(n + 1) * TX].rearrange("p (t e) -> p t e", e=XP)

        probs, key, first, second, both, cum, place = (r3(n) for n in range(7))
        r1 = [rw[:, 7 * TX + n * T:7 * TX + (n + 1) * T] for n in range(4)]
        rxT = work[:, 7 * TX + 4 * T:7 * TX + 4 * T + 2 * DC * P].rearrange("p (k c n) -> p k c n", k=2, c=DC)
        lane_hot = [norm_all[0:P, 0:T * L].rearrange("p (t q) -> p t q", q=L),
                    norm_all[0:P, T * L:2 * T * L].rearrange("p (t q) -> p t q", q=L)]
        block_hot = [accf[:, k * T * 2 * NBLK:(k + 1) * T * 2 * NBLK].rearrange("p (t f j) -> p t f j", f=2, j=NBLK)
                     for k in range(2)]
        expert_rev = sb("expert_rev", [P, XP])

        ps = ctx.enter_context(nc.psum_tensor("ps", [L, 8, 512], f32))

        s_edges = sem("s_edges")
        s_x = sem("s_x")
        s_x2 = sem("s_x2")
        s_w = sem("s_w")
        s_zfill = sem("s_zfill")
        s_recs = sem("s_recs")
        s_support_out = sem("s_support_out")
        s_wup = sem("s_wup")
        s_const = sem("s_const")
        s_pool = sem("s_pool")
        s_dve = sem("s_dve")
        s_act = sem("s_act")
        count_ready = sem("count_ready")
        base_ready = sem("base_ready")
        slots_ready = sem("slots_ready")
        zeros_ready = sem("zeros_ready")
        scattered = [sem("scattered0"), sem("scattered1")]
        var_ready = sem("var_ready")
        std_ready = sem("std_ready")
        xn_ready = sem("xn_ready")
        xnT_psum = sem("xnT_psum")
        xnT_ready = sem("xnT_ready")
        proj_ready = sem("proj_ready")
        proj_free_act = sem("proj_free_act")
        proj_free_dve = sem("proj_free_dve")
        q_shifted = sem("q_shifted")
        q_exped = sem("q_exped")
        q_ready = sem("q_ready")
        support_ready = sem("support_ready")
        kmaxT_ready = sem("kmaxT_ready")
        kmaxb_ready = sem("kmaxb_ready")
        kshift_psum = sem("kshift_psum")
        kshift_ready = sem("kshift_ready")
        k_shifted = sem("k_shifted")
        k_exped = sem("k_exped")
        ctx_ready = sem("ctx_ready")
        ctxT_ready = sem("ctxT_ready")
        mixw_psum = sem("mixw_psum")
        mixw_ready = sem("mixw_ready")
        q_staged = sem("q_staged")
        qT_psum = sem("qT_psum")
        qT_ready = sem("qT_ready")
        mix_psum = sem("mix_psum")
        mix_copied = sem("mix_copied")
        arena_free = sem("arena_free")
        gidx_ready = sem("gidx_ready")
        map_ready = sem("map_ready")
        gathered = [sem(f"gathered{k}") for k in range(GU)]
        onehot_ready = sem("onehot_ready")
        chunk_summed = sem("chunk_summed")
        chunk_added = sem("chunk_added")
        norm_ready = sem("norm_ready")
        rT_psum = sem("rT_psum")
        rT_ready = sem("rT_ready")
        logits_ready = sem("logits_ready")
        pair_count_ready = sem("pair_count_ready")
        pair_base_ready = sem("pair_base_ready")
        expert_map_ready = sem("expert_map_ready")
        x1_ready = sem("x1_ready")
        x1_out = sem("x1_out")
        norm_out = sem("norm_out")
        pairs_hot = sem("pairs_hot")
        pairs_placed = sem("pairs_placed")
        blocks_ready = sem("blocks_ready")
        x_loaded = [sem("x_loaded0"), sem("x_loaded1")]
        xt_psum = sem("xt_psum")
        xt_ready = sem("xt_ready")
        h_ready = sem("h_ready")
        silu_ready = sem("silu_ready")
        g_ready = sem("g_ready")
        gT_psum = sem("gT_psum")
        gT_act = sem("gT_act")
        gT_dve = sem("gT_dve")
        y_psum = sem("y_psum")
        y_ready = sem("y_ready")
        y_added = sem("y_added")
        s_out = sem("s_out")
        s_idle = sem("s_idle")

        def apart(eng):
            eng.sem_inc(s_idle, 1)

        class Steps:

            def __init__(self, eng, s):
                self.eng, self.s, self.n = eng, s, 0

            def mark(self, ins):
                ins.then_inc(self.s, 1)
                self.n = self.n + 1
                return self.n

            def wait(self, but=0):
                self.eng.wait_ge(self.s, self.n - but)

            def link(self, ins):
                self.mark(ins)
                self.wait()

            def link_apart(self, ins):
                self.link(ins)
                apart(self.eng)

            @contextmanager
            def loop(self, start, end, per):
                base = self.n
                with self.eng.Fori(start, end) as i:
                    self.n = base + (i - start) * per
                    yield i
                self.n = base + (end - start) * per

        block = ctx.enter_context(nc.Block())

        support_rows = support_table.rearrange("(p t) d -> p (t d)", t=T)
        edge_rows = edge_table.rearrange("(q c) r -> q (c r)", c=NCH)
        x_rows = x.rearrange("(p t) d -> p (t d)", t=T)
        out_rows = x_out[0:N, :].rearrange("(p t) d -> p (t d)", t=T)
        norm_rows = norm_table.rearrange("(p t) d -> p (t d)", t=T)
        SPLIT = P // 16 * 16

        @block.sync
        def _(sp):
            sp.dma_start(src_i, src.rearrange("(p c) -> p c", c=C)).then_inc(s_edges, 16)
            sp.dma_start(dst_i, dst.rearrange("(p c) -> p c", c=C)).then_inc(s_edges, 16)
            sp.dma_start(wgt, edge_weight.rearrange("(p c) -> p c", c=C)).then_inc(s_edges, 16)
            sp.dma_start(accf[0:SPLIT], x_rows[0:SPLIT]).then_inc(s_x, 16)
            sp.dma_start(accf[SPLIT:P], x_rows[SPLIT:P]).then_inc(s_x2, 16)
            sp.dma_start(wqkvg[:, :, 0:D], w_gnn.rearrange("(c p) n -> p c n", p=L)).then_inc(s_w, 16)
            wq = w_qkv.rearrange("(c p) n -> p c n", p=L)
            sp.dma_start(wqkvg[:, :, D:2 * D], wq[:, :, 2 * D:3 * D]).then_inc(s_w, 16)
            sp.dma_start(wqkvg[:, :, 2 * D:4 * D], wq[:, :, 0:2 * D]).then_inc(s_w, 16)
            sp.dma_start(wout_sb, w_out.rearrange("(c p) n -> p c n", p=L)).then_inc(s_w, 16)
            sp.dma_start(wr_sb, w_router.rearrange("(c p) n -> p c n", p=L)).then_inc(s_w, 16)
            sp.dma_start(gamma_sb, gamma).then_inc(s_w, 16)
            sp.wait_ge(zeros_ready, 1)
            sp.dma_start(edge_rows, zeros[:, 0:NCH * 3]).then_inc(s_zfill, 16)
            sp.dma_start(x_out[N:N + L, :], zeros[:, 0:D]).then_inc(s_zfill, 16)
            sp.wait_ge(support_ready, T)
            sp.dma_start(support_rows[0:SPLIT], normf[0:SPLIT]).then_inc(s_support_out, 16)
            sp.dma_start(support_rows[SPLIT:P], normf[SPLIT:P]).then_inc(s_support_out, 16)
            sp.wait_ge(arena_free, 1)
            sp.wait_ge(s_zfill, 32)
            for e in range(XP):
                n = DC * 2 * H
                sp.dma_start(wup[:, e * n:(e + 1) * n], w_up[:, e, :, :].rearrange("p c n -> p (c n)"))\
                  .then_inc(s_wup, 16)
                n = HC * D
                sp.dma_start(wdn[:, e * n:(e + 1) * n], w_down[:, e, :, :].rearrange("p c n -> p (c n)"))\
                  .then_inc(s_wup, 16)
            sp.wait_ge(scattered[0], 16 * SA * STURNS)
            sp.wait_ge(scattered[1], 16 * SB_ * STURNS)
            sp.dma_start(rec_in, edge_rows).then_inc(s_recs, 16)

            sp.wait_ge(x1_ready, 1)
            sp.dma_start(out_rows[0:SPLIT], accf[0:SPLIT]).then_inc(x1_out, 16)
            sp.dma_start(out_rows[SPLIT:P], accf[SPLIT:P]).then_inc(x1_out, 16)
            for g in range(T // GB):
                sp.wait_ge(norm_ready, GB * (g + 1))
                cols = slice(g * GB * D, (g + 1) * GB * D)
                sp.dma_start(norm_rows[0:SPLIT, cols], normf[0:SPLIT, cols]).then_inc(norm_out, 16)
                sp.dma_start(norm_rows[SPLIT:P, cols], normf[SPLIT:P, cols]).then_inc(norm_out, 16)
            sp.wait_ge(y_added, 16 * NBLK)

        @block.gpsimd
        def _(pool):
            steps = Steps(pool, s_pool)
            pool.iota(tile_no, [[1, T]], base=0, channel_multiplier=0,
                      allow_small_or_imprecise_dtypes=True).then_inc(s_const, 1)
            steps.mark(pool.memset(upper[:], 1.0))
            steps.mark(pool.memset(ident[:], 0.0))
            steps.wait()
            pool.affine_select(out=upper[:], in_=upper[:], compare_op=ALU.is_gt, fill=0.0, base=0,
                               pattern=[[1, P]], channel_multiplier=-1).then_inc(s_const, 1)
            pool.affine_select(out=ident[:], in_=ident[:], compare_op=ALU.not_equal, fill=1.0, base=0,
                               pattern=[[-1, L]], channel_multiplier=1).then_inc(s_const, 1)
            pool.memset(ones[:], 1.0).then_inc(s_const, 1)
            pool.iota(chunk_no, [[1, NCH]], base=0, channel_multiplier=0,
                      allow_small_or_imprecise_dtypes=True).then_inc(s_const, 1)
            pool.iota(block_no, [[1, NBLK]], base=0, channel_multiplier=0,
                      allow_small_or_imprecise_dtypes=True).then_inc(s_const, 1)
            pool.iota(node_no, [[1, T]], base=1, channel_multiplier=T,
                      allow_small_or_imprecise_dtypes=True).then_inc(s_const, 1)
            pool.iota(lane, [[0, 1]], base=0, channel_multiplier=1,
                      allow_small_or_imprecise_dtypes=True).then_inc(s_const, 1)
            pool.iota(lane_row[:], [[1, L]], base=0, channel_multiplier=0,
                      allow_small_or_imprecise_dtypes=True).then_inc(s_const, 1)
            pool.iota(expert_rev[:], [[-1, XP]], base=XP, channel_multiplier=0,
                      allow_small_or_imprecise_dtypes=True).then_inc(s_const, 1)
            pool.memset(zeros, 0.0).then_inc(zeros_ready, 1)

            pool.wait_ge(slots_ready, 2)
            pool.wait_ge(s_zfill, 32)

            def scatter_half(i, h, first):
                n, at0 = (SA, 0) if h == 0 else (SB_, SA)
                if not first:
                    pool.wait_ge(scattered[h], 16 * n * i)
                steps.mark(pool.tensor_copy(stage_slot[h][:], slot_i[:, bass.ds(i * SU + at0, n)]))
                steps.mark(pool.tensor_copy(stage_rec[h][:], rec[:, bass.ds((i * SU + at0) * 3, n * 3)]))
                steps.wait()
                apart(pool)
                for c in range(n):
                    pool.indirect_dma_start(
                        out=edge_table, out_offset=bass.IndirectOffsetOnAxis(ap=stage_slot[h][:, c:c + 1], axis=0),
                        in_=stage_rec[h][:, 3 * c:3 * c + 3], in_offset=None).then_inc(scattered[h], 16)

            for h in range(2):
                scatter_half(0, h, True)
            with steps.loop(1, STURNS, 4) as i:
                for h in range(2):
                    scatter_half(i, h, False)

            pool.wait_ge(gidx_ready, 1)
            pool.wait_ge(s_support_out, 32)
            with steps.loop(0, GTURNS, 2) as i:
                for h in range(2):
                    top = GU // 2 * (h + 1)
                    pool.wait_ge(chunk_summed, i * GU + top)
                    steps.link_apart(pool.tensor_copy(stage_gidx[h][:], gidx[:, bass.ds(i * GU + GU // 2 * h, GU // 2)]))
                    for k in range(GU // 2 * h, top):
                        pool.indirect_dma_start(
                            out=gbuf[:, k, :], out_offset=None, in_=support_table,
                            in_offset=bass.IndirectOffsetOnAxis(ap=stage_gidx[h][:, k % 4:k % 4 + 1], axis=0))\
                            .then_inc(gathered[k], 16)

            def take(j, k):
                steps.link_apart(pool.tensor_copy(stage_token[k][:], block_token[:, bass.ds(j, 1)]))
                pool.indirect_dma_start(
                    out=X[k], out_offset=None, in_=norm_table,
                    in_offset=bass.IndirectOffsetOnAxis(ap=stage_token[k][:], axis=0)).then_inc(x_loaded[k], 16)

            def give(j, k, first):
                if not first:
                    pool.wait_ge(y_added, 16 * j)
                pool.wait_ge(y_ready, j + 1)
                steps.link_apart(pool.tensor_copy(stage_dest[k][:], block_dest[:, bass.ds(j, 1)]))
                pool.indirect_dma_start(
                    out=x_out, out_offset=bass.IndirectOffsetOnAxis(ap=stage_dest[k][:], axis=0),
                    in_=Y[k], in_offset=None, compute_op=ALU.add).then_inc(y_added, 16)

            def turn(j, k, first, more):
                if more:
                    pool.wait_ge(xt_psum, j + 1)
                    take(j + 2, k)
                give(j, k, first)

            pool.wait_ge(blocks_ready, 1)
            pool.wait_ge(norm_out, 16 * 2 * (T // GB))
            pool.wait_ge(x1_out, 32)
            take(0, 0)
            take(1, 1)
            turn(0, 0, True, True)
            turn(1, 1, False, True)
            with steps.loop(1, NBLK // 2 - 1, 4) as i:
                for k in range(2):
                    turn(2 * i + k, k, False, True)
            turn(NBLK - 2, 0, False, False)
            turn(NBLK - 1, 1, False, False)

        @block.scalar
        def _(act):
            steps = Steps(act, s_act)

            def copy(out, in_):
                return act.copy(out, in_)

            act.wait_ge(s_edges, 48)
            rec3 = rec.rearrange("p (c r) -> p c r", r=3)
            copy(rec3[:, :, 0], dst_i)
            copy(rec3[:, :, 2], wgt).then_inc(slots_ready, 1)

            act.sem_inc(proj_free_act, 2)
            act.wait_ge(var_ready, 1)
            act.activation(rstd, rstd, ACT.Sqrt).then_inc(std_ready, 1)

            def tile_T(bank):
                return ps[:, bank, 0:DC * P].rearrange("p (c n) -> p c n", c=DC)

            def copy_T(t, k):
                act.wait_ge(xnT_psum, 2 + t + 1)
                copy(row_T[k], tile_T(3 * k)).then_inc(xnT_ready, 1)

            def projections(t, k, more):
                if more:
                    copy_T(t + 1, 1 - k)
                act.wait_ge(proj_ready, t + 1)
                copy(normf[:, bass.ds(t * D, D)], ps[0:P, 3 * k + 1, 0:D]).then_inc(support_ready, 1)
                copy(V[:, bass.ds(t * D, D)], ps[0:P, 3 * k + 1, D:2 * D]).then_inc(proj_free_act, 1)
                act.wait_ge(q_shifted, t + 1)
                act.activation(Q[:, bass.ds(t * D, D)], Q[:, bass.ds(t * D, D)], ACT.Exp).then_inc(q_exped, 1)

            copy_T(0, 0)
            with act.Fori(0, T // 2) as i:
                projections(2 * i, 0, True)
                projections(2 * i + 1, 1, True)
            projections(T - 1, 0, False)
            act.wait_ge(kshift_psum, 1)
            copy(kshift, ps[0:P, 1, 0:D]).then_inc(kshift_ready, 1)
            with act.Fori(0, T) as t:
                act.wait_ge(k_shifted, t + 1)
                act.activation(K[:, bass.ds(t * D, D)], K[:, bass.ds(t * D, D)], ACT.Exp).then_inc(k_exped, 1)
            act.wait_ge(q_ready, T)

            def stage_q(t, k):
                copy(row_in[k], Q[:, bass.ds(t * D, D)]).then_inc(q_staged, 1)

            def mixed(t, k):
                act.wait_ge(mix_psum, t + 1)
                act.activation(K[:, bass.ds(t * D, D)], ps[0:P, 3 * k + 1, 0:D], ACT.Copy).then_inc(mix_copied, 1)

            def attend(t, k, before, more):
                if more:
                    stage_q(t + 1, 1 - k)
                act.wait_ge(qT_psum, t + 1)
                copy(row_T[k], tile_T(3 * k)).then_inc(qT_ready, 1)
                if before:
                    mixed(t - 1, 1 - k)

            stage_q(0, 0)
            attend(0, 0, False, True)
            with act.Fori(0, T // 2 - 1) as i:
                attend(2 * i + 1, 1, True, True)
                attend(2 * i + 2, 0, True, True)
            attend(T - 2, 1, True, True)
            attend(T - 1, 0, True, False)
            mixed(T - 1, 0)
            act.wait_ge(var_ready, 2)
            act.activation(rstd, rstd, ACT.Sqrt).then_inc(std_ready, 1)

            act.wait_ge(var_ready, 3)
            act.activation(rstd, rstd, ACT.Sqrt).then_inc(std_ready, 1)

            def router_copy(t, k):
                act.wait_ge(rT_psum, t + 1)
                copy(rxT[:, k, :, :], ps[:, 4 + k, 0:DC * P].rearrange("p (c n) -> p c n", c=DC)).then_inc(rT_ready, 1)

            with act.Fori(0, T // 2) as i:
                router_copy(2 * i, 0)
                router_copy(2 * i + 1, 1)
            router_copy(T - 1, 0)
            act.wait_ge(var_ready, 4)
            act.activation(probs, probs, ACT.Exp).then_inc(std_ready, 1)

            def xt_copy(j):
                act.wait_ge(xt_psum, j + 1)
                copy(XT, ps[:, 4, 0:DC * L].rearrange("p (c n) -> p c n", c=DC)).then_inc(xt_ready, 1)

            def do_silu(j):
                act.wait_ge(h_ready, j + 1)
                act.activation(silu, ps[:, 0:2, 0:HB], ACT.Silu).then_inc(silu_ready, 1)

            def gt_copy(j):
                act.wait_ge(gT_psum, j + 1)
                copy(GT[:, 0:4, :], ps[:, 5, :].rearrange("p (c n) -> p c n", n=L)).then_inc(gT_act, 1)

            xt_copy(0)
            with act.Fori(0, NBLK - 1) as j:
                do_silu(j)
                xt_copy(j + 1)
                gt_copy(j)
            do_silu(NBLK - 1)
            gt_copy(NBLK - 1)

        @block.tensor
        def _(pe):
            pe.wait_ge(s_const, 10)
            pe.wait_ge(count_ready, 1)
            pe.matmul(ps[0:P, 3, 0:T], upper[:], count, start=True, stop=True)
            pe.matmul(ps[:, 3, 32:32 + T], ones[:], count, start=True, stop=True).then_inc(base_ready, 1)

            def transpose_rows(bank, rows):
                for c in range(DC):
                    mm = pe.transpose(ps[:, bank, c * P:(c + 1) * P], rows[:, c * L:(c + 1) * L], ident[0:P, 0:P])
                return mm

            pe.sem_inc(xnT_psum, 2)
            pe.wait_ge(s_w, 16 * 6)

            def transpose_x(t, k):
                pe.wait_ge(xn_ready, t + 1)
                transpose_rows(3 * k, row_in[k]).then_inc(xnT_psum, 1)

            def project(t, k, more):
                if more:
                    transpose_x(t + 1, 1 - k)
                pe.wait_ge(xnT_ready, t + 1)
                pe.wait_ge(proj_free_act, t + 1)
                pe.wait_ge(proj_free_dve, t + 1)
                for n in range(2):
                    for c in range(DC):
                        mm = pe.matmul(ps[0:P, 3 * k + 1 + n, :], row_T[k][:, c, :], wqkvg[:, c, n * 512:(n + 1) * 512],
                                       start=(c == 0), stop=(c == DC - 1))
                mm.then_inc(proj_ready, 1)

            transpose_x(0, 0)
            with pe.Fori(0, T // 2) as i:
                project(2 * i, 0, True)
                project(2 * i + 1, 1, True)
            project(T - 1, 0, False)
            pe.wait_ge(kmaxT_ready, 1)
            for c in range(DC):
                mm = pe.transpose(ps[:, 0, c * P:(c + 1) * P], kmax[:, c * L:(c + 1) * L], ident[0:P, 0:P])
            mm.then_inc(kmaxT_ready, 1)
            pe.wait_ge(kmaxb_ready, 1)
            for c in range(DC):
                mm = pe.matmul(ps[0:P, 1, c * L:(c + 1) * L], kmaxb[:, c, :], ident[:], start=True, stop=True)
            mm.then_inc(kshift_psum, 1)

            def context(t, start, stop):
                pe.wait_ge(k_exped, t + 1)
                for c in range(DC):
                    kk = K[:, bass.ds(t * D + c * L, L)]
                    pe.matmul(ps[:, 4 + c, 0:L], V[:, bass.ds(t * D + c * L, L)], kk, start=start, stop=stop)
                    mm = pe.matmul(ps[:, 6 + c, 0:1], kk, ones[:, 0:1], start=start, stop=stop)
                return mm

            for t in range(T):
                mm = context(t, t == 0, t == T - 1)
            mm.then_inc(ctx_ready, 1)
            pe.wait_ge(ctxT_ready, 1)
            for c in range(DC):
                mm = pe.matmul(ps[:, 1, c * D:(c + 1) * D], ctxT[:, c, :], wout_sb[:, c, :], start=True, stop=True)
            mm.then_inc(mixw_psum, 1)
            pe.wait_ge(mixw_ready, 1)

            def transpose_q(t, k):
                pe.wait_ge(q_staged, t + 1)
                transpose_rows(3 * k, row_in[k]).then_inc(qT_psum, 1)

            def mix(t, k, more):
                if more:
                    transpose_q(t + 1, 1 - k)
                pe.wait_ge(qT_ready, t + 1)
                for c in range(DC):
                    mm = pe.matmul(ps[0:P, 3 * k + 1, 0:D], row_T[k][:, c, :], mix_w[:, c, :],
                                   start=(c == 0), stop=(c == DC - 1))
                mm.then_inc(mix_psum, 1)

            transpose_q(0, 0)
            mix(0, 0, True)
            mix(1, 1, True)
            with pe.Fori(1, T // 2) as i:
                for k in range(2):
                    pe.wait_ge(mix_copied, 2 * i + k - 1)
                    mix(2 * i + k, k, True)
            pe.wait_ge(mix_copied, T - 2)
            mix(T - 1, 0, False)

            pe.sem_inc(chunk_summed, GU)
            with pe.Fori(0, GTURNS) as i:
                for k in range(GU):
                    pe.wait_ge(onehot_ready, i * GU + k + 1)
                    pe.wait_ge(gathered[k], 16 * (i + 1))
                    pe.wait_ge(chunk_added, i * GU + k + 1)
                    pe.matmul(ps[0:P, k % QK, 0:D], onehot[:, k, :], gbuf[:, k, :], start=True, stop=True)\
                        .then_inc(chunk_summed, 1)

            def transpose_x1(t):
                pe.wait_ge(norm_ready, t + 1)
                transpose_rows(4 + t % 2, norm[:, t, :]).then_inc(rT_psum, 1)

            transpose_x1(0)
            for t in range(T):
                if t + 1 < T:
                    transpose_x1(t + 1)
                pe.wait_ge(rT_ready, t + 1)
                for c in range(DC):
                    mm = pe.matmul(ps[0:P, 6, t * XP:(t + 1) * XP], rxT[:, t % 2, c, :], wr_sb[:, c, :],
                                   start=(c == 0), stop=(c == DC - 1))
                mm.then_inc(logits_ready, 1)
            pe.wait_ge(pair_count_ready, 1)
            pe.matmul(ps[0:P, 7, 0:XP], upper[:], count[:, 0:XP], start=True, stop=True)
            pe.matmul(ps[:, 7, 32:32 + XP], ones[:], count[:, 0:XP], start=True, stop=True).then_inc(pair_base_ready, 1)

            for k in range(2):
                pe.wait_ge(pairs_hot, k + 1)
                for t in range(T):
                    mm = pe.matmul(ps[:, 3, 0:2 * NBLK], lane_hot[k][:, t, :],
                                   block_hot[k][:, t, :, :].rearrange("p f j -> p (f j)"),
                                   start=(k == 0 and t == 0), stop=(k == 1 and t == T - 1))
            mm.then_inc(pairs_placed, 1)

            pe.wait_ge(expert_map_ready, 1)
            pe.wait_ge(s_wup, 16 * 2 * XP)

            def expert(j):
                return pe.value_load(block_expert[0:1, bass.ds(j, 1)], min_val=0, max_val=XP - 1)

            def x_transpose(j, k, turn):
                pe.wait_ge(x_loaded[k], 16 * turn)
                for c in range(DC):
                    mm = pe.transpose(ps[:, 4, c * L:(c + 1) * L], X[k][:, c * L:(c + 1) * L], ident[:])
                mm.then_inc(xt_psum, 1)

            def up(j, e):
                pe.wait_ge(xt_ready, j + 1)
                for n in range(4):
                    for c in range(DC):
                        mm = pe.matmul(ps[:, n, 0:HB], XT[:, c, :],
                                       wup[:, bass.ds(e * (DC * 2 * H) + (c * 2 * H + n * HB), HB)],
                                       start=(c == 0), stop=(c == DC - 1))
                mm.then_inc(h_ready, 1)

            def g_transpose(j, k):
                pe.wait_ge(g_ready, j + 1)
                for c in range(HC):
                    w = L if c < HC - 1 else HL
                    mm = pe.transpose(ps[0:w, 5 + c // 4, (c % 4) * L:(c % 4 + 1) * L], G[k][:, c * L:c * L + w], ident[:])
                mm.then_inc(gT_psum, 1)

            def down(j, e):
                pe.wait_ge(gT_act, j + 1)
                pe.wait_ge(gT_dve, j + 1)
                for c in range(HC):
                    w = L if c < HC - 1 else HL
                    mm = pe.matmul(ps[:, 7, 0:D], GT[0:w, c, :], wdn[0:w, bass.ds(e * (HC * D) + c * D, D)],
                                   start=(c == 0), stop=(c == HC - 1))
                mm.then_inc(y_psum, 1)

            def turn(j, k, loads, more):
                before = expert(j - 1)
                e = expert(j)
                up(j, e)
                if more:
                    x_transpose(j + 1, 1 - k, loads)
                if not isinstance(j, int) or j >= 2:
                    pe.wait_ge(y_ready, j - 1)
                down(j - 1, before)
                g_transpose(j, k)

            x_transpose(0, 0, 1)
            up(0, expert(0))
            x_transpose(1, 1, 1)
            g_transpose(0, 0)
            turn(1, 1, 2, True)
            turn(2, 0, 2, True)
            with pe.Fori(1, NBLK // 2 - 1) as i:
                turn(2 * i + 1, 1, i + 2, True)
                turn(2 * i + 2, 0, i + 2, True)
            turn(NBLK - 1, 1, 0, False)
            pe.wait_ge(y_ready, NBLK - 1)
            down(NBLK - 1, expert(NBLK - 1))

        @block.vector
        def _(dve):
            v = nc.vector
            steps = Steps(dve, s_dve)
            v.memset(rank, 0.0).then_inc(s_dve, 1)
            v.memset(kmax, -3.0e38).then_inc(s_dve, 1)
            v.memset(ctxT, 0.0).then_inc(s_dve, 1)
            steps.n = 3
            dve.sem_inc(proj_free_dve, 2)
            dve.sem_inc(chunk_added, QK)

            dve.wait_ge(s_edges, 48)
            dve.wait_ge(s_const, 10)
            steps.link(v.tensor_scalar(tmp, src_i, 1.0 / T, -0.5 + 0.5 / T, ALU.mult, ALU.add))
            steps.link(v.tensor_scalar(row_of, tmp, ROUND, -ROUND, ALU.add, ALU.add))
            steps.link(v.scalar_tensor_tensor(tile_of, row_of, -float(T), src_i, ALU.mult, ALU.add))
            v.tensor_copy(rec.rearrange("p (c r) -> p c r", r=3)[:, :, 1], row_of).then_inc(s_dve, 1)
            steps.n += 1
            with steps.loop(0, T // GB, GB) as g:
                for k in range(GB):
                    b = g * GB + k
                    steps.mark(v.tensor_scalar(mask[k], tile_of, tile_no[0:P, bass.ds(b, 1)], 0.0, ALU.is_equal,
                                               ALU.add, accum_out=count[:, bass.ds(b, 1)]))
                steps.wait()
            dve.sem_inc(count_ready, 1)

            def block_counts(nb, bank):
                steps.link(v.tensor_scalar(blocks[:, 0:nb], ps[:, bank, 32:32 + nb], 1.0 / L, 0.5 - 0.5 / L,
                                           ALU.mult, ALU.add))
                steps.link(v.tensor_scalar(blocks[:, 0:nb], blocks[:, 0:nb], ROUND, -ROUND, ALU.add, ALU.add))
                steps.link(v.tensor_tensor_scan(blocks_to[:, 0:nb], blocks[:, 0:nb], blocks[:, 0:nb], 0.0,
                                                ALU.add, ALU.max))
                steps.link(v.tensor_tensor(first_slot[:, 0:nb], blocks_to[0:P, 0:nb], blocks[0:P, 0:nb], ALU.subtract))
                steps.link(v.scalar_tensor_tensor(first_slot[:, 0:nb], first_slot[:, 0:nb], float(L),
                                                  ps[0:P, bank, 0:nb], ALU.mult, ALU.add))

            dve.wait_ge(base_ready, 1)
            block_counts(T, 3)
            with steps.loop(0, T // GB, 3 * GB) as g:
                for k in range(GB):
                    steps.mark(v.tensor_scalar(mask[k], tile_of, tile_no[0:P, bass.ds(g * GB + k, 1)], None,
                                               ALU.is_equal))
                steps.wait()
                for k in range(GB + 1):
                    if k < GB:
                        steps.mark(v.tensor_tensor_scan(ps[0:P, 3 + k, 0:C], mask[k], mask[k],
                                                        first_slot[:, bass.ds(g * GB + k, 1)], ALU.add, ALU.max))
                    if k > 0:
                        steps.wait(but=1 if k < GB else 0)
                        apart(dve)
                        steps.mark(v.copy_predicated(rank, mask[k - 1], ps[0:P, 2 + k, 0:C]))
                steps.wait()
            steps.link(v.tensor_scalar(rank, rank, -1.0, None, ALU.add))
            steps.link(v.tensor_scalar(tmp, rank, 1.0 / L, -0.5 + 0.5 / L, ALU.mult, ALU.add))
            steps.link(v.tensor_scalar(tmp, tmp, ROUND, -ROUND, ALU.add, ALU.add))
            steps.link(v.scalar_tensor_tensor(tmp2, tmp, -float(L), rank, ALU.mult, ALU.add))
            v.scalar_tensor_tensor(slot_i, tmp2, float(NCH), tmp, ALU.mult, ALU.add).then_inc(slots_ready, 1)

            dve.wait_ge(s_x, 16)
            dve.wait_ge(s_x2, 16)

            def tile_stats(t):
                return stats6[:, bass.ds(t * 6, 6)]

            def deviation(turn):
                steps.mark(v.tensor_tensor(mean, stats[:, :, 1], stats[:, :, 4], ALU.add))
                steps.mark(v.tensor_tensor(spread, stats[:, :, 1], stats[:, :, 4], ALU.subtract))
                steps.link(v.tensor_tensor(rstd, stats[:, :, 2], stats[:, :, 5], ALU.add))
                steps.mark(v.tensor_scalar(mean, mean, 0.5, None, ALU.mult))
                steps.mark(v.tensor_tensor(spread, spread, spread, ALU.mult))
                steps.link(v.tensor_scalar(rstd, rstd, 1.0 / D, EPS, ALU.mult, ALU.add))
                v.scalar_tensor_tensor(rstd, spread, 0.25, rstd, ALU.mult, ALU.add).then_inc(var_ready, 1)
                dve.wait_ge(std_ready, turn)
                steps.link(v.reciprocal(rstd, rstd))

            def acc_tile(t):
                return accf[:, bass.ds(t * D, D)]

            with steps.loop(0, T, 1) as t:
                steps.mark(v.bn_stats(tile_stats(t), acc_tile(t)))
            steps.wait()
            deviation(1)

            def by_head(a):
                return a.rearrange("p (h d) -> p h d", h=HEADS)

            def normalise(t, k):
                dve.wait_ge(xnT_psum, t + 1)
                v.tensor_scalar(row_in[k], acc_tile(t), mean[:, bass.ds(t, 1)], rstd[:, bass.ds(t, 1)],
                                ALU.subtract, ALU.mult).then_inc(xn_ready, 1)

            def q_divide(t):
                dve.wait_ge(q_exped, t + 1)
                apart(dve)
                qt = by_head(Q[:, bass.ds(t * D, D)])
                steps.link(v.tensor_reduce(qsum, qt, AX.X, ALU.add))
                steps.link(v.reciprocal(qrec, qsum))
                v.tensor_tensor(qt, qt, qrec.unsqueeze(2).broadcast_to([P, HEADS, DH]), ALU.mult).then_inc(q_ready, 1)

            def use_projections(t, k, before, more):
                if more:
                    normalise(t + 1, 1 - k)
                dve.wait_ge(proj_ready, t + 1)
                q, kk = ps[0:P, 3 * k + 2, 0:D], ps[0:P, 3 * k + 2, D:2 * D]
                steps.mark(v.tensor_reduce(qmax, by_head(q), AX.X, ALU.max))
                steps.link(v.tensor_copy(K[:, bass.ds(t * D, D)], kk))
                v.tensor_tensor(by_head(Q[:, bass.ds(t * D, D)]), by_head(q),
                                qmax.unsqueeze(2).broadcast_to([P, HEADS, DH]), ALU.subtract).then_inc(q_shifted, 1)
                steps.link(v.tensor_tensor(kmax, kk, kmax, ALU.max))
                dve.sem_inc(proj_free_dve, 1)
                if before:
                    q_divide(t - 1)

            normalise(0, 0)
            use_projections(0, 0, False, True)
            with steps.loop(0, T // 2 - 1, 10) as i:
                use_projections(2 * i + 1, 1, True, True)
                use_projections(2 * i + 2, 0, True, True)
            use_projections(T - 2, 1, True, True)
            use_projections(T - 1, 0, True, False)
            q_divide(T - 1)
            dve.sem_inc(kmaxT_ready, 1)

            dve.wait_ge(kmaxT_ready, 2)
            steps.link(v.tensor_reduce(kneg, ps[:, 0, 0:DC * P].rearrange("p (c n) -> p c n", c=DC), AX.X, ALU.max))
            v.tensor_copy(kmaxb, kneg.unsqueeze(2).broadcast_to([L, DC, P])).then_inc(kmaxb_ready, 1)
            dve.wait_ge(kshift_ready, 1)
            with dve.Fori(0, T) as t:
                kt = K[:, bass.ds(t * D, D)]
                v.tensor_tensor(kt, kt, kshift, ALU.subtract).then_inc(k_shifted, 1)

            dve.wait_ge(ctx_ready, 1)
            for c in range(DC):
                for h in range(HPC):
                    r = slice(h * DH, (h + 1) * DH)
                    steps.mark(v.tensor_copy(ctxT[r, c, r], ps[r, 4 + c, r]))
            steps.wait()
            dve.sem_inc(ctxT_ready, 1)
            for c in range(DC):
                steps.link(v.reciprocal(krec[:, c:c + 1], ps[:, 6 + c, 0:1]))
            steps.link(v.tensor_scalar(krec, krec, SCALE, None, ALU.mult))
            dve.wait_ge(mixw_psum, 1)
            for c in range(DC):
                steps.mark(v.tensor_scalar(mix_w[:, c, :], ps[:, 1, c * D:(c + 1) * D], krec[:, c:c + 1], None, ALU.mult))
            steps.wait()
            dve.sem_inc(mixw_ready, 1)

            with steps.loop(0, T, 1) as t:
                dve.wait_ge(mix_copied, t + 1)
                steps.mark(v.bn_stats(tile_stats(t), K[:, bass.ds(t * D, D)]))
            steps.wait()
            deviation(2)
            with steps.loop(0, T // GB, 3 * GB) as g:
                rows = [K[:, bass.ds((g * GB + r) * D, D)] for r in range(GB)]
                for r in range(GB):
                    t = g * GB + r
                    steps.mark(v.tensor_scalar(rows[r], rows[r], mean[:, bass.ds(t, 1)], rstd[:, bass.ds(t, 1)],
                                               ALU.subtract, ALU.mult))
                steps.wait()
                for r in range(GB):
                    steps.mark(v.tensor_tensor(rows[r], rows[r], gamma_sb, ALU.mult))
                steps.wait()
                for r in range(GB):
                    steps.mark(v.tensor_tensor(acc_tile(g * GB + r), acc_tile(g * GB + r), rows[r], ALU.add))
            steps.wait()

            def bucket_map(out_i, number, total, nb):
                steps.link(v.memset(total, 0.0))
                for b in range(nb - 1):
                    steps.link(v.scalar_tensor_tensor(total, number, blocks_to[0:1, b:b + 1], total,
                                                      ALU.is_ge, ALU.add))
                steps.link(v.tensor_copy(out_i, total))

            bucket_map(chunk_tile[:], chunk_no, chunk_acc, T)
            dve.sem_inc(arena_free, 1)

            dve.wait_ge(s_recs, 16)
            dve.wait_ge(s_support_out, 32)
            rin = rec_in.rearrange("p (c r) -> p c r", r=3)
            v.tensor_copy(gidx, rin[:, :, 0]).then_inc(gidx_ready, 1)

            def edge_rows_of(c, k):
                v.tensor_scalar(onehot[:, k, :], lane_no, rec_in[:, bass.ds(c * 3 + 1, 1)],
                                rec_in[:, bass.ds(c * 3 + 2, 1)], ALU.is_equal, ALU.mult).then_inc(onehot_ready, 1)

            def add_blocks(i, more):
                _, tiles = nc.values_load_multi_w_load_instructions(
                    chunk_tile[0:1, bass.ds(i * GU, GU)], engines=(mybir.EngineType.DVE,), min_val=0, max_val=T - 1)
                for k in range(GU):
                    dve.wait_ge(chunk_summed, GU + i * GU + k + 1)
                    a = accf[:, bass.ds(tiles[k] * D, D)]
                    v.tensor_tensor(a, a, ps[0:P, k % QK, 0:D], ALU.add).then_inc(chunk_added, 1)
                    if more:
                        edge_rows_of((i + 1) * GU + k, k)
                    dve.wait_ge(chunk_added, QK + i * GU + k + 1)

            for k in range(GU):
                edge_rows_of(k, k)
            with dve.Fori(0, GTURNS - 1) as i:
                add_blocks(i, True)
            add_blocks(GTURNS - 1, False)
            dve.sem_inc(x1_ready, 1)

            with steps.loop(0, T, 1) as t:
                steps.mark(v.bn_stats(tile_stats(t), acc_tile(t)))
            steps.wait()
            deviation(3)

            with dve.Fori(0, T) as t:
                v.tensor_scalar(normf[:, bass.ds(t * D, D)], acc_tile(t), mean[:, bass.ds(t, 1)],
                                rstd[:, bass.ds(t, 1)], ALU.subtract, ALU.mult).then_inc(norm_ready, 1)
            dve.wait_ge(logits_ready, T)
            lg = ps[0:P, 6, 0:TX].rearrange("p (t e) -> p t e", e=XP)

            def over_experts(a):
                return a.unsqueeze(2).broadcast_to([P, T, XP])

            def over_tiles(a):
                return a.unsqueeze(1).broadcast_to([P, T, XP])

            steps.link(v.tensor_reduce(r1[0], lg, AX.X, ALU.max))
            v.tensor_tensor(probs, lg, over_experts(r1[0]), ALU.subtract).then_inc(var_ready, 1)
            dve.wait_ge(std_ready, 4)
            steps.link(v.tensor_reduce(r1[0], probs, AX.X, ALU.add))
            steps.link(v.reciprocal(r1[1], r1[0]))
            steps.link(v.tensor_tensor(probs, probs, over_experts(r1[1]), ALU.mult))

            def pick(mine, top):
                steps.link(v.tensor_reduce(top, probs, AX.X, ALU.max))
                steps.link(v.tensor_tensor(key, probs, over_experts(top), ALU.is_equal))
                steps.link(v.tensor_tensor(key, key, over_tiles(expert_rev[:]), ALU.mult))
                steps.link(v.tensor_reduce(r1[0], key, AX.X, ALU.max))
                steps.link(v.tensor_tensor(mine, key, over_experts(r1[0]), ALU.is_equal))

            pick(first, r1[1])
            steps.link(v.scalar_tensor_tensor(probs, first, -2.0, probs, ALU.mult, ALU.add))
            pick(second, r1[2])
            steps.link(v.tensor_tensor(r1[0], r1[1], r1[2], ALU.add))
            steps.link(v.tensor_scalar(r1[0], r1[0], 1e-9, None, ALU.add))
            steps.link(v.reciprocal(r1[3], r1[0]))
            steps.mark(v.tensor_tensor(gate[:, 0, :], r1[1], r1[3], ALU.mult))
            steps.mark(v.tensor_tensor(gate[:, 1, :], r1[2], r1[3], ALU.mult))
            steps.wait()
            steps.link(v.tensor_tensor(both, first, second, ALU.add))
            for e in range(XP):
                steps.mark(v.tensor_tensor_scan(cum[:, :, e], both[:, :, e], both[:, :, e], 0.0, ALU.add, ALU.max))
            steps.wait()
            v.tensor_copy(count[:, 0:XP], cum[:, T - 1, :]).then_inc(pair_count_ready, 1)
            dve.wait_ge(pair_base_ready, 1)
            block_counts(XP, 7)
            steps.link(v.tensor_scalar(first_slot[:, 0:XP], first_slot[:, 0:XP], -1.0, None, ALU.add))
            steps.link(v.tensor_tensor(place, cum, over_tiles(first_slot[:, 0:XP]), ALU.add))
            dve.wait_ge(norm_out, 16 * 2 * (T // GB))
            dve.wait_ge(x1_out, 32)
            slot, pair_block = r1[0], r1[1]
            for k, mine in enumerate((first, second)):
                steps.link(v.tensor_tensor(key, mine, place, ALU.mult))
                steps.link(v.tensor_reduce(slot, key, AX.X, ALU.add))
                steps.link(v.tensor_scalar(pair_block, slot, 1.0 / L, -0.5 + 0.5 / L, ALU.mult, ALU.add))
                steps.link(v.tensor_scalar(pair_block, pair_block, ROUND, -ROUND, ALU.add, ALU.add))
                steps.mark(v.scalar_tensor_tensor(slot, pair_block, -float(L), slot, ALU.mult, ALU.add))
                steps.link(v.tensor_tensor(block_hot[k][:, :, 0, :], block_no.unsqueeze(1).broadcast_to([P, T, NBLK]),
                                           pair_block.unsqueeze(2).broadcast_to([P, T, NBLK]), ALU.is_equal))
                steps.mark(v.tensor_tensor(lane_hot[k], lane_row[0:P].unsqueeze(1).broadcast_to([P, T, L]),
                                           slot.unsqueeze(2).broadcast_to([P, T, L]), ALU.is_equal))
                steps.link(v.tensor_tensor(block_hot[k][:, :, 1, :], block_hot[k][:, :, 0, :],
                                           gate[:, k, :].unsqueeze(2).broadcast_to([P, T, NBLK]), ALU.mult))
                steps.link(v.tensor_tensor(block_hot[k][:, :, 0, :], block_hot[k][:, :, 0, :],
                                           node_no.unsqueeze(2).broadcast_to([P, T, NBLK]), ALU.mult))
                dve.sem_inc(pairs_hot, 1)
            bucket_map(block_expert[:], block_no[0:1], block_acc, XP)
            dve.sem_inc(expert_map_ready, 1)
            dve.wait_ge(pairs_placed, 1)
            steps.mark(v.tensor_copy(block_gate, ps[:, 3, NBLK:2 * NBLK]))
            steps.link(v.tensor_scalar(block_node, ps[:, 3, 0:NBLK], -1.0, None, ALU.add))
            steps.mark(v.tensor_scalar(block_empty, block_node, 0.0, float(N + 1), ALU.is_lt, ALU.mult))
            steps.link(v.tensor_scalar(block_token, block_node, 0.0, None, ALU.max))
            steps.link(v.tensor_tensor(block_node, block_node, block_empty, ALU.add))
            steps.link(v.tensor_scalar(block_empty, block_empty, 1.0 / (N + 1), lane, ALU.mult, ALU.mult))
            v.tensor_tensor(block_dest, block_node, block_empty, ALU.add).then_inc(blocks_ready, 1)

            def gated(j, k):
                dve.wait_ge(silu_ready, j + 1)
                v.tensor_tensor(G[k].rearrange("p (a n) -> p a n", a=2), ps[:, 2:4, 0:HB], silu, ALU.mult)\
                 .then_inc(g_ready, 1)

            def gt_copy(j):
                dve.wait_ge(gT_psum, j + 1)
                v.tensor_copy(GT[:, 4, :], ps[:, 6, 0:L])
                v.tensor_copy(GT[0:HL, 5, :], ps[0:HL, 6, L:2 * L]).then_inc(gT_dve, 1)

            def y_copy(j, k, first):
                dve.wait_ge(y_psum, j + 1)
                if not first:
                    dve.wait_ge(y_added, 16 * (j - 1))
                v.tensor_scalar(Y[k], ps[:, 7, 0:D], block_gate[:, bass.ds(j, 1)], None, ALU.mult)\
                 .then_inc(y_ready, 1)

            def turn(j, k, first):
                gated(j, k)
                y_copy(j - 1, 1 - k, first)
                gt_copy(j)

            gated(0, 0)
            gt_copy(0)
            turn(1, 1, True)
            turn(2, 0, True)
            with dve.Fori(1, NBLK // 2 - 1) as i:
                turn(2 * i + 1, 1, False)
                turn(2 * i + 2, 0, False)
            turn(NBLK - 1, 1, False)
            y_copy(NBLK - 1, 1, False)


def kernel(x, src, dst, edge_weight, L0_gnn_W, L0_mix_Wqkv, L0_mix_Wout, L0_mix_gamma,
           L0_ffn_router_w, L0_ffn_w1, L0_ffn_w2, L0_ffn_w3):
    import numpy as np
    import concourse.bacc as _bacc
    from concourse import mybir as _mybir
    from concourse.bass_utils import run_bass_kernel_spmd as _run

    L = 128
    N, D = x.shape
    E = src.shape[0]
    XP, H, _ = L0_ffn_w1.shape
    HC = -(-H // L)
    T = 25
    w1, w2, w3 = (np.asarray(a) for a in (L0_ffn_w1, L0_ffn_w2, L0_ffn_w3))
    w_up = np.concatenate([w1, w3], axis=1).transpose(2, 0, 1).reshape(D // L, L, XP, 2 * H).transpose(1, 2, 0, 3)
    w_down = np.zeros((XP, HC * L, D), w2.dtype)
    w_down[:, :H, :] = w2.transpose(0, 2, 1)
    w_down = w_down.reshape(XP, HC, L, D).transpose(2, 0, 1, 3)
    ins = {
        "x": np.asarray(x), "src": np.asarray(src), "dst": np.asarray(dst), "edge_weight": np.asarray(edge_weight),
        "w_gnn": np.asarray(L0_gnn_W), "w_qkv": np.asarray(L0_mix_Wqkv), "w_out": np.asarray(L0_mix_Wout),
        "gamma": np.broadcast_to(np.asarray(L0_mix_gamma), (N // T, D)), "w_router": np.asarray(L0_ffn_router_w).T,
        "w_up": w_up, "w_down": w_down,
    }
    nc = _bacc.Bacc("TRN2", target_bir_lowering=False, num_devices=1)
    f32 = _mybir.dt.float32
    arrays, args = {}, []
    for name, a in ins.items():
        a = np.ascontiguousarray(a)
        arrays[f"in_{name}"] = a
        args.append(nc.dram_tensor(f"in_{name}", a.shape, _mybir.dt.from_np(a.dtype), kind="ExternalInput").ap())
    args.append(nc.dram_tensor("x_out", (N + L, D), f32, kind="ExternalOutput").ap())
    chunks = -(-((E + T * (L - 1)) // L) // 8) * 8
    args.append(nc.dram_tensor("support_table", (N, D), f32, kind="Internal").ap())
    args.append(nc.dram_tensor("edge_table", (L * chunks, 3), f32, kind="Internal").ap())
    args.append(nc.dram_tensor("norm_table", (N, D), f32, kind="Internal").ap())
    gps_layer_program(nc, *args)
    r = _run(nc, [arrays], core_ids=[0])
    return r.results[0]["x_out"][:N]
```

```python
import concourse.bass as bass
from concourse import mybir
from contextlib import ExitStack, contextmanager


def gps_layer_program(nc, x, src, dst, edge_weight, w_gnn, w_qkv, w_out, gamma, w_router, w_up, w_down,
                      x_out, support_table, edge_table, norm_table):
    f32, i32, u16 = mybir.dt.float32, mybir.dt.int32, mybir.dt.uint16
    f32r = mybir.dt.float32r
    f16, bf16 = mybir.dt.float16, mybir.dt.bfloat16
    ALU, ACT, AX = mybir.AluOpType, mybir.ActivationFunctionType, mybir.AxisListType

    L = 128
    N, D = x.shape
    T = 25
    P = N // T
    E = src.shape[0]
    C = E // P
    DC = D // L
    HEADS, DH = 8, 32
    HPC = L // DH
    XP = w_router.shape[1]
    H = w_up.shape[3] // 2
    HB = H // 2
    HC = -(-H // L)
    HL = H - (HC - 1) * L
    EPS = 1e-05
    SCALE = DH ** -0.5
    ROUND = 1.5 * 2.0 ** 23

    GU = 8
    GTURNS = -(-((E + T * (L - 1)) // L) // GU)
    NCH = GTURNS * GU
    NBLK = (2 * N + XP * (L - 1)) // L
    SA, SB_ = 15, 15
    SU = SA + SB_
    HK = 5
    NB = HK
    PEC = T * HK
    STURNS = (C - PEC) // SU
    SFIRST = 2
    LOW = 2048.0
    ROW = 128
    WCUT = 2
    WPIECES = XP * (DC + 1) * WCUT
    QK = 4
    GB = 5
    assert HK % NB == 0 and T % 4 == 1 and NBLK % 4 == 0
    assert STURNS * SU + PEC == C and P * T == N and P * C == E and T % GB == 0 and T % 2 and NBLK % 2 == 0

    ctx = ExitStack()
    with ctx:
        def sb(name, shape, dt=f32):
            return ctx.enter_context(nc.sbuf_tensor(name, shape, dt))

        def sem(name):
            return ctx.enter_context(nc.semaphore(name))

        state_place = -(-nc.sbuf_base // 32) * 32
        state = sb("state", [L, 2 * T * D])
        acc = state[0:P, 0:T * D].rearrange("p (t d) -> p t d", d=D)
        norm_all = state[:, T * D:2 * T * D]
        gbuf = norm_all[:, 0:GU * D].rearrange("p (k n) -> p k n", k=GU)
        onehot = norm_all[:, GU * D:GU * (D + P)].rearrange("p (k n) -> p k n", k=GU)
        accf = state[0:P, 0:T * D]
        normf = norm_all[0:P, :]
        ident = sb("ident", [L, L])
        upper = sb("upper", [P, P])
        ones = sb("ones", [L, L])
        lane_row = sb("lane_row", [L, L])
        lane_no = lane_row[:, 0:P]
        chunk_tile = sb("chunk_tile", [1, NCH], i32)
        block_expert = sb("block_expert", [1, NBLK], i32)
        small = sb("small", [L, 960])

        WUP, WDN = XP * DC * 2 * H, XP * HC * D
        arena_place = -(-nc.sbuf_base // 32) * 32
        arena = sb("arena", [L, WUP + WDN])
        wup = arena[:, 0:WUP]
        wdn = nc.alloc_sbuf_tensor_at("wdn", [L, WDN], f32, offset=arena_place + 4 * WUP)
        wdn_high = nc.alloc_sbuf_tensor_at("wdn_high", [L, WDN], f32r, offset=state_place)
        wdn_low = nc.alloc_sbuf_tensor_at("wdn_low", [L, WDN], f32r, offset=arena_place + 4 * WUP)
        at = [0]

        def carve(cols, rows=L):
            a = at[0]
            at[0] += cols
            assert at[0] <= WUP + WDN
            return arena[0:rows, a:a + cols]

        src_i, dst_i = carve(C, P).bitcast(i32), carve(C, P).bitcast(i32)
        wgt = carve(C, P)
        row_of = carve(C, P)
        rank = carve(C, P)
        tmp = carve(C, P)
        tmp2 = carve(C, P)
        hot_place = carve(NB * (L + NCH) // 2)
        zeros = carve(NCH * 2)
        chunk_no = carve(NCH, P)
        chunk_no16 = carve(NCH // 2, P).bitcast(f16)
        lane16 = carve(L // 2, P).bitcast(f16)
        zero16 = carve(L // 2, P).bitcast(f16)
        parts = carve(5 * PEC, P).rearrange("p (n c) -> p n c", c=PEC)
        part16 = carve((PEC + 1) // 2, P).bitcast(bf16)[:, 0:PEC]
        chunk_reached = carve(NCH, T)
        wqkvg = carve(DC * 4 * D).rearrange("p (c n) -> p c n", c=DC)
        wout_sb = carve(DC * D).rearrange("p (c n) -> p c n", c=DC)
        gamma_sb = carve(D, P)
        row_in = [carve(D, P), carve(D, P)]
        row_T = [carve(DC * P).rearrange("p (c n) -> p c n", c=DC) for _ in range(2)]
        Q = carve(T * D, P)
        K = carve(T * D, P)
        MW = C // 2 + 1
        assert T * MW <= T * D
        masks = K[:, 0:T * MW].bitcast(f16)
        mask = [masks[:, b * 2 * MW:b * 2 * MW + C] for b in range(T)]
        tile_of16 = carve(C // 2 + 1, P).bitcast(f16)[:, 0:C]
        V = carve(T * DC * (L + 1), P)
        V4 = V.rearrange("p (t c n) -> p t c n", c=DC, n=L + 1)
        kmax = carve(D, P)
        kshift = carve(D, P)
        kmaxb = carve(DC * P).rearrange("p (c n) -> p c n", c=DC)
        context_sb = carve(DC * L).rearrange("p (c n) -> p c n", c=DC)
        ctxT = carve(DC * L).rearrange("p (c n) -> p c n", c=DC)
        mix_w = carve(DC * D).rearrange("p (c n) -> p c n", c=DC)
        WORK = -(-(DC * L + 2 * H + 2 * D) // 8) * 8 + 2 * HC * L
        work_place = -(-nc.sbuf_base // 32) * 32
        work = sb("work", [L, WORK])
        rec_in = work[:, 0:NCH * 2]
        gidx = work[:, NCH * 2:NCH * 3].bitcast(i32)
        edge_row = work[:, NCH * 3:NCH * 4]
        edge_target = work[:, NCH * 4:NCH * 5]

        def hot_buffers(place, at, cols, dt):
            return place[0:P, at:at + NB * cols // 2].bitcast(dt).rearrange("p (k q) -> p k q", q=cols)

        assert NB * 5 * L // 2 <= NCH * 5
        hot_row = [hot_buffers(work, n * NB * L // 2, L, bf16 if n < 4 else f16) for n in range(5)]
        hot_one = hot_buffers(hot_place, 0, L, f16)
        hot_chunk = hot_buffers(hot_place, NB * L // 2, NCH, f16)
        rec = work[0:P, NCH * 5:NCH * 5 + 2 * C]
        slot_i = work[0:P, NCH * 5 + 2 * C:NCH * 5 + 3 * C].bitcast(i32)
        wat = [0]

        def wcarve(cols):
            a = wat[0]
            wat[0] += cols
            assert wat[0] <= WORK - 2 * HC * L
            return work[:, a:a + cols]

        X = [state[:, WDN + k * D:WDN + (k + 1) * D] for k in range(2)]
        assert WDN + 2 * D <= 2 * T * D
        XT = wcarve(DC * L).rearrange("p (c n) -> p c n", c=DC)
        silu = wcarve(H).rearrange("p (a n) -> p a n", a=2)
        G = wcarve(H)
        GT_high, GT_low = (nc.alloc_sbuf_tensor_at(name, [L, HC, L], f32r, offset=work_place + 4 * (WORK - n * HC * L))
                           for name, n in (("GT_high", 2), ("GT_low", 1)))
        Y = [wcarve(D), wcarve(D)]

        stage_slot = [sb("stage_slot0", [P, SA], i32), sb("stage_slot1", [P, SB_], i32)]
        stage_rec = [sb("stage_rec0", [P, SA * 2]), sb("stage_rec1", [P, SB_ * 2])]
        stage_gidx = [sb("stage_gidx0", [L, GU // 2], i32), sb("stage_gidx1", [L, GU // 2], i32)]
        stage_token = [sb("stage_token0", [L, 1], i32), sb("stage_token1", [L, 1], i32)]
        stage_dest = [sb("stage_dest0", [L, 1], i32), sb("stage_dest1", [L, 1], i32)]

        so = [0]

        def s_carve(cols, rows=L):
            a = so[0]
            so[0] += cols
            assert so[0] <= 960
            return small[0:rows, a:a + cols]

        tile_no = s_carve(T)
        count = s_carve(T, P)
        first_slot = s_carve(T, P)
        blocks = s_carve(T)
        blocks_to = s_carve(T)
        stats6 = s_carve(6 * T, P)
        stats = stats6.rearrange("p (t s) -> p t s", s=6)
        mean = s_carve(T, P)
        spread = s_carve(T, P)
        rstd = s_carve(T, P)
        qmax = s_carve(HEADS, P)
        qsum = s_carve(HEADS, P)
        qrec = s_carve(HEADS, P)
        kneg = s_carve(DC)
        krec = s_carve(DC)
        wr_sb = s_carve(DC * XP).rearrange("p (c n) -> p c n", c=DC)
        gate = s_carve(2 * T, P).rearrange("p (k t) -> p k t", k=2)
        node_no = s_carve(T, P)
        lane = s_carve(1)
        block_no = s_carve(NBLK, P)
        block_reached = s_carve(NBLK, XP)
        small_map = s_carve(2)
        block_token = s_carve(NBLK).bitcast(i32)
        block_dest = s_carve(NBLK).bitcast(i32)
        block_gate = s_carve(NBLK)
        block_node = s_carve(NBLK)
        block_empty = s_carve(NBLK)

        TX = T * XP
        rw = work[0:P, 0:7 * TX + 4 * T]

        def r3(n):
            return rw[:, n * TX:(n + 1) * TX].rearrange("p (t e) -> p t e", e=XP)

        PT = 5
        probs, key, first, second, both, cum, place = (r3(n) for n in range(7))
        r1 = [rw[:, 7 * TX + n * T:7 * TX + (n + 1) * T] for n in range(4)]
        keys = [key, both]
        logits = place
        pair_slot = rw[:, 7 * TX:7 * TX + 2 * T].rearrange("p (k t) -> p k t", k=2)
        pair_block = rw[:, 7 * TX + 2 * T:7 * TX + 4 * T].rearrange("p (k t) -> p k t", k=2)
        RP = 2
        rxT = work[:, 7 * TX + 4 * T:7 * TX + 4 * T + 2 * RP * DC * P].rearrange("p (k c n) -> p k c n", k=2, n=P)
        lane_hot = [norm_all[0:P, 0:T * L].rearrange("p (t q) -> p t q", q=L),
                    norm_all[0:P, T * L:2 * T * L].rearrange("p (t q) -> p t q", q=L)]
        block_hot = [accf[:, k * T * 2 * NBLK:(k + 1) * T * 2 * NBLK].rearrange("p (t f j) -> p t f j", f=2, j=NBLK)
                     for k in range(2)]
        pair_tiles = [slice(t0, min(t0 + PT, T)) for t0 in range(0, T, PT)]
        expert_rev = sb("expert_rev", [P, XP])

        ps = ctx.enter_context(nc.psum_tensor("ps", [L, 8, 512], f32))

        s_edges = sem("s_edges")
        s_x = sem("s_x")
        s_x2 = sem("s_x2")
        s_w = sem("s_w")
        s_zfill = sem("s_zfill")
        s_recs = sem("s_recs")
        s_support_out = sem("s_support_out")
        s_wup = sem("s_wup")
        s_const = sem("s_const")
        s_pool = sem("s_pool")
        s_dve = sem("s_dve")
        s_act = sem("s_act")
        count_ready = sem("count_ready")
        base_ready = sem("base_ready")
        slots_ready = sem("slots_ready")
        rec_weights_ready = sem("rec_weights_ready")
        zeros_ready = sem("zeros_ready")
        parts_ready = sem("parts_ready")
        edge_hot = sem("edge_hot")
        edge_scaled = sem("edge_scaled")
        edges_placed = sem("edges_placed")
        edge_psum_ready = sem("edge_psum_ready")
        scattered = [sem("scattered0"), sem("scattered1")]
        var_ready = sem("var_ready")
        std_ready = sem("std_ready")
        xn_ready = sem("xn_ready")
        xnT_psum = sem("xnT_psum")
        xnT_ready = sem("xnT_ready")
        proj_ready = sem("proj_ready")
        proj_free_act = sem("proj_free_act")
        proj_free_dve = sem("proj_free_dve")
        q_shifted = sem("q_shifted")
        q_exped = sem("q_exped")
        q_ready = sem("q_ready")
        support_ready = sem("support_ready")
        kmaxT_ready = sem("kmaxT_ready")
        kmaxb_ready = sem("kmaxb_ready")
        kshift_psum = sem("kshift_psum")
        kshift_ready = sem("kshift_ready")
        k_shifted = sem("k_shifted")
        k_exped = sem("k_exped")
        ctx_ready = sem("ctx_ready")
        ctx_masked = sem("ctx_masked")
        ctxT_ready = sem("ctxT_ready")
        mixw_psum = sem("mixw_psum")
        mixw_ready = sem("mixw_ready")
        qT_psum = sem("qT_psum")
        qT_ready = sem("qT_ready")
        mix_psum = sem("mix_psum")
        mix_copied = sem("mix_copied")
        gidx_ready = sem("gidx_ready")
        gidx_staged = sem("gidx_staged")
        map_ready = sem("map_ready")
        map_step = sem("map_step")
        gathered = [sem(f"gathered{k}") for k in range(GU)]
        onehot_ready = sem("onehot_ready")
        chunk_summed = sem("chunk_summed")
        chunk_added = sem("chunk_added")
        norm_ready = sem("norm_ready")
        router_sum_ready = sem("router_sum_ready")
        rT_psum = sem("rT_psum")
        rT_ready = sem("rT_ready")
        logits_ready = sem("logits_ready")
        pair_count_ready = sem("pair_count_ready")
        pair_base_ready = sem("pair_base_ready")
        expert_map_ready = sem("expert_map_ready")
        x1_ready = sem("x1_ready")
        x1_out = sem("x1_out")
        norm_out = sem("norm_out")
        pair_blocks_hot = sem("pair_blocks_hot")
        pair_lanes_hot = sem("pair_lanes_hot")
        pair_values_hot = sem("pair_values_hot")
        pairs_placed = sem("pairs_placed")
        blocks_ready = sem("blocks_ready")
        wdn_rounded = sem("wdn_rounded")
        wdn_split = sem("wdn_split")
        x_loaded = [sem("x_loaded0"), sem("x_loaded1")]
        xt_psum = sem("xt_psum")
        xt_ready = sem("xt_ready")
        h_ready = sem("h_ready")
        silu_ready = sem("silu_ready")
        g_ready = sem("g_ready")
        gT_psum = sem("gT_psum")
        gT_act = sem("gT_act")
        gT_dve = sem("gT_dve")
        y_psum = sem("y_psum")
        y_ready = sem("y_ready")
        y_added = sem("y_added")
        s_idle = sem("s_idle")

        def apart(eng):
            eng.sem_inc(s_idle, 1)

        class Steps:

            def __init__(self, eng, s):
                self.eng, self.s, self.n = eng, s, 0

            def mark(self, ins):
                ins.then_inc(self.s, 1)
                self.n = self.n + 1
                return self.n

            def wait(self, but=0):
                self.eng.wait_ge(self.s, self.n - but)

            def link(self, ins):
                self.mark(ins)
                self.wait()

            def link_apart(self, ins):
                self.link(ins)
                apart(self.eng)

            @contextmanager
            def loop(self, start, end, per):
                base = self.n
                with self.eng.Fori(start, end) as i:
                    self.n = base + (i - start) * per
                    yield i
                self.n = base + (end - start) * per

        block = ctx.enter_context(nc.Block())

        support_rows = support_table.rearrange("(p t) d -> p (t d)", t=T)
        edge_rows = edge_table.rearrange("(q c) r -> q (c r)", c=NCH)
        x_rows = x.rearrange("(p t) d -> p (t d)", t=T)
        out_rows = x_out[0:N, :].rearrange("(p t) d -> p (t d)", t=T)
        norm_rows = norm_table.rearrange("(p t) d -> p (t d)", t=T)
        SPLIT = P // 16 * 16

        def split_wdn(eng, experts):
            for e in experts:
                at = slice(e * HC * D, (e + 1) * HC * D)
                eng.wait_ge(wdn_rounded, e + 1)
                eng.tensor_tensor(wdn_low[:, at], wdn[:, at], wdn_high[:, at], ALU.subtract).then_inc(wdn_split, 1)

        @block.sync
        def _(sp):
            sp.dma_start(src_i, src.rearrange("(p c) -> p c", c=C)).then_inc(s_edges, 16)
            sp.dma_start(dst_i, dst.rearrange("(p c) -> p c", c=C)).then_inc(s_edges, 16)
            sp.dma_start(wgt, edge_weight.rearrange("(p c) -> p c", c=C)).then_inc(s_edges, 16)
            sp.dma_start(accf[0:SPLIT], x_rows[0:SPLIT]).then_inc(s_x, 16)
            sp.dma_start(accf[SPLIT:P], x_rows[SPLIT:P]).then_inc(s_x2, 16)
            sp.dma_start(wqkvg[:, :, 0:D], w_gnn.rearrange("(c p) n -> p c n", p=L)).then_inc(s_w, 16)
            wq = w_qkv.rearrange("(c p) n -> p c n", p=L)
            sp.dma_start(wqkvg[:, :, D:2 * D], wq[:, :, 2 * D:3 * D]).then_inc(s_w, 16)
            sp.dma_start(wqkvg[:, :, 2 * D:4 * D], wq[:, :, 0:2 * D]).then_inc(s_w, 16)
            sp.dma_start(wout_sb, w_out.rearrange("(c p) n -> p c n", p=L)).then_inc(s_w, 16)
            sp.dma_start(wr_sb, w_router.rearrange("(c p) n -> p c n", p=L)).then_inc(s_w, 16)
            sp.dma_start(gamma_sb, gamma).then_inc(s_w, 16)
            sp.wait_ge(zeros_ready, 1)
            sp.dma_start(edge_rows, zeros[:, 0:NCH * 2]).then_inc(s_zfill, 16)
            sp.dma_start(x_out[N:N + L, :], zeros[:, 0:D]).then_inc(s_zfill, 16)
            sp.wait_ge(support_ready, T)
            sp.dma_start(support_rows[0:SPLIT], normf[0:SPLIT]).then_inc(s_support_out, 16)
            sp.dma_start(support_rows[SPLIT:P], normf[SPLIT:P]).then_inc(s_support_out, 16)
            sp.wait_ge(scattered[0], 16 * SA * STURNS)
            sp.wait_ge(scattered[1], 16 * SB_ * STURNS)
            sp.wait_ge(edge_psum_ready, 1)
            sp.dma_start(rec_in, edge_rows).then_inc(s_recs, 16)
            pieces = []
            for e in range(XP):
                n, m = 2 * H // WCUT, HC * D // WCUT
                for c in range(DC):
                    for h in range(WCUT):
                        at = (e * DC + c) * 2 * H + h * n
                        pieces.append((wup[:, at:at + n], w_up[:, e, c, h * n:(h + 1) * n]))
                for h in range(WCUT):
                    at = slice(h * HC // WCUT, (h + 1) * HC // WCUT)
                    pieces.append((wdn[:, e * HC * D + h * m:e * HC * D + (h + 1) * m],
                                   w_down[:, e, at, :].rearrange("p c n -> p (c n)")))
            for n, (place, weights) in enumerate(pieces):
                sp.wait_ge(chunk_added, QK + n * (NCH // (WPIECES + 1)) + 1)
                sp.dma_start(place, weights).then_inc(s_wup, 16)

            sp.wait_ge(x1_ready, 1)
            sp.dma_start(out_rows[0:SPLIT], accf[0:SPLIT]).then_inc(x1_out, 16)
            sp.dma_start(out_rows[SPLIT:P], accf[SPLIT:P]).then_inc(x1_out, 16)
            for g in range(T // GB):
                sp.wait_ge(norm_ready, GB * (g + 1))
                cols = slice(g * GB * D, (g + 1) * GB * D)
                sp.dma_start(norm_rows[0:SPLIT, cols], normf[0:SPLIT, cols]).then_inc(norm_out, 16)
                sp.dma_start(norm_rows[SPLIT:P, cols], normf[SPLIT:P, cols]).then_inc(norm_out, 16)
            sp.wait_ge(y_added, 16 * NBLK)

        @block.gpsimd
        def _(pool):
            steps = Steps(pool, s_pool)
            pool.iota(tile_no, [[1, T]], base=0, channel_multiplier=0,
                      allow_small_or_imprecise_dtypes=True).then_inc(s_const, 1)
            steps.mark(pool.memset(upper[:], 1.0))
            steps.mark(pool.memset(ident[:], 0.0))
            steps.wait()
            pool.affine_select(out=upper[:], in_=upper[:], compare_op=ALU.is_gt, fill=0.0, base=0,
                               pattern=[[1, P]], channel_multiplier=-1).then_inc(s_const, 1)
            pool.affine_select(out=ident[:], in_=ident[:], compare_op=ALU.not_equal, fill=1.0, base=0,
                               pattern=[[-1, L]], channel_multiplier=1).then_inc(s_const, 1)
            pool.memset(ones[:], 1.0).then_inc(s_const, 1)
            pool.iota(chunk_no, [[1, NCH]], base=0, channel_multiplier=0,
                      allow_small_or_imprecise_dtypes=True).then_inc(s_const, 1)
            pool.iota(block_no, [[1, NBLK]], base=0, channel_multiplier=0,
                      allow_small_or_imprecise_dtypes=True).then_inc(s_const, 1)
            pool.iota(node_no, [[1, T]], base=1, channel_multiplier=T,
                      allow_small_or_imprecise_dtypes=True).then_inc(s_const, 1)
            pool.iota(lane, [[0, 1]], base=0, channel_multiplier=1,
                      allow_small_or_imprecise_dtypes=True).then_inc(s_const, 1)
            pool.iota(lane_row[:], [[1, L]], base=0, channel_multiplier=0,
                      allow_small_or_imprecise_dtypes=True).then_inc(s_const, 1)
            pool.iota(expert_rev[:], [[-1, XP]], base=XP, channel_multiplier=0,
                      allow_small_or_imprecise_dtypes=True).then_inc(s_const, 1)
            pool.memset(zeros, 0.0).then_inc(zeros_ready, 1)

            pool.wait_ge(rec_weights_ready, 1)
            pool.wait_ge(slots_ready, 1)
            pool.wait_ge(s_zfill, 32)

            def scatter_half(i, h, first):
                n, at0 = (SA, 0) if h == 0 else (SB_, SA)
                if not first:
                    pool.wait_ge(scattered[h], 16 * n * i)
                steps.mark(pool.tensor_copy(stage_slot[h][:], slot_i[:, bass.ds(i * SU + at0, n)]))
                steps.mark(pool.tensor_copy(stage_rec[h][:], rec[:, bass.ds((i * SU + at0) * 2, n * 2)]))
                steps.wait()
                apart(pool)
                for c in range(n):
                    pool.indirect_dma_start(
                        out=edge_table, out_offset=bass.IndirectOffsetOnAxis(ap=stage_slot[h][:, c:c + 1], axis=0),
                        in_=stage_rec[h][:, 2 * c:2 * c + 2], in_offset=None).then_inc(scattered[h], 16)

            for h in range(2):
                scatter_half(0, h, True)
            with steps.loop(1, SFIRST, 4) as i:
                for h in range(2):
                    scatter_half(i, h, False)
            pool.wait_ge(slots_ready, 2)
            with steps.loop(SFIRST, STURNS, 4) as i:
                for h in range(2):
                    scatter_half(i, h, False)

            pool.wait_ge(s_support_out, 32)
            with pool.Fori(0, GTURNS) as i:
                for h in range(2):
                    top = GU // 2 * (h + 1)
                    pool.wait_ge(gidx_staged, 2 * i + h + 1)
                    apart(pool)
                    for k in range(GU // 2 * h, top):
                        pool.indirect_dma_start(
                            out=gbuf[:, k, :], out_offset=None, in_=support_table,
                            in_offset=bass.IndirectOffsetOnAxis(ap=stage_gidx[h][:, k % 4:k % 4 + 1], axis=0))\
                            .then_inc(gathered[k], 16)

            def take(j, k):
                steps.link_apart(pool.tensor_copy(stage_token[k][:], block_token[:, bass.ds(j, 1)]))
                pool.indirect_dma_start(
                    out=X[k], out_offset=None, in_=norm_table,
                    in_offset=bass.IndirectOffsetOnAxis(ap=stage_token[k][:], axis=0)).then_inc(x_loaded[k], 16)

            def give(j, k, first):
                if not first:
                    pool.wait_ge(y_added, 16 * j)
                pool.wait_ge(y_ready, j + 1)
                steps.link_apart(pool.tensor_copy(stage_dest[k][:], block_dest[:, bass.ds(j, 1)]))
                pool.indirect_dma_start(
                    out=x_out, out_offset=bass.IndirectOffsetOnAxis(ap=stage_dest[k][:], axis=0),
                    in_=Y[k], in_offset=None, compute_op=ALU.add).then_inc(y_added, 16)

            def turn(j, k, first, more):
                if more:
                    pool.wait_ge(xt_psum, j + 2)
                    take(j + 3, 1 - k)
                give(j, k, first)

            for k in range(2):
                for n, at in enumerate(pair_tiles):
                    pool.wait_ge(pair_blocks_hot, k * len(pair_tiles) + n + 1)
                    hot = block_hot[k][:, at, :, :]
                    shape = [P, at.stop - at.start, NBLK]
                    steps.link(pool.tensor_tensor(hot[:, :, 1, :], hot[:, :, 0, :],
                                                  gate[:, k, at].unsqueeze(2).broadcast_to(shape), ALU.mult))
                    pool.tensor_tensor(hot[:, :, 0, :], hot[:, :, 0, :],
                                       node_no[:, at].unsqueeze(2).broadcast_to(shape), ALU.mult)\
                        .then_inc(pair_values_hot, 1)

            pool.wait_ge(blocks_ready, 1)
            pool.wait_ge(norm_out, 16 * 2 * (T // GB))
            pool.wait_ge(x1_out, 32)
            take(0, 0)
            take(1, 1)
            pool.wait_ge(xt_psum, 1)
            take(2, 0)
            split_wdn(pool, [4, 5])
            turn(0, 0, True, True)
            turn(1, 1, False, True)
            with steps.loop(1, NBLK // 2 - 2, 4) as i:
                for k in range(2):
                    turn(2 * i + k, k, False, True)
            turn(NBLK - 4, 0, False, True)
            turn(NBLK - 3, 1, False, False)
            turn(NBLK - 2, 0, False, False)
            turn(NBLK - 1, 1, False, False)

        @block.scalar
        def _(act):
            steps = Steps(act, s_act)

            def copy(out, in_):
                return act.copy(out, in_)

            act.wait_ge(s_edges, 48)
            copy(rec.rearrange("p (c r) -> p c r", r=2)[:, :, 1], wgt).then_inc(rec_weights_ready, 1)

            act.sem_inc(proj_free_act, 2)
            act.wait_ge(var_ready, 1)
            act.activation(rstd, rstd, ACT.Sqrt).then_inc(std_ready, 1)

            def tile_T(bank):
                return ps[:, bank, 0:DC * P].rearrange("p (c n) -> p c n", c=DC)

            def copy_T(t, k):
                act.wait_ge(xnT_psum, 2 + t + 1)
                copy(row_T[k], tile_T(3 * k)).then_inc(xnT_ready, 1)

            def projections(t, k, more):
                if more:
                    copy_T(t + 1, 1 - k)
                for c in range(HK):
                    act.wait_ge(edge_hot, (t * HK + c + 1) * 4)
                    for n in range(2, 5):
                        act.activation(hot_row[n][:, c % NB, :], hot_one[:, c % NB, :], ACT.Copy,
                                       scale=parts[:, n, bass.ds(t * HK + c, 1)]).then_inc(edge_scaled, 1)
                act.wait_ge(proj_ready, t + 1)
                copy(normf[:, bass.ds(t * D, D)], ps[0:P, 3 * k + 1, 0:D]).then_inc(support_ready, 1)
                copy(V4[:, bass.ds(t, 1), :, 0:L],
                     ps[0:P, 3 * k + 1, D:2 * D].rearrange("p (a c n) -> p a c n", a=1, c=DC))\
                    .then_inc(proj_free_act, 1)
                act.wait_ge(q_shifted, t + 1)
                act.activation(Q[:, bass.ds(t * D, D)], Q[:, bass.ds(t * D, D)], ACT.Exp).then_inc(q_exped, 1)

            copy_T(0, 0)
            with act.Fori(0, T // 2) as i:
                projections(2 * i, 0, True)
                projections(2 * i + 1, 1, True)
            projections(T - 1, 0, False)
            act.wait_ge(kshift_psum, 1)
            copy(kshift, ps[0:P, 1, 0:D]).then_inc(kshift_ready, 1)
            with act.Fori(0, T // GB) as g:
                for r in range(GB):
                    t = g * GB + r
                    act.wait_ge(k_shifted, t + 1)
                    act.activation(K[:, bass.ds(t * D, D)], K[:, bass.ds(t * D, D)], ACT.Exp).then_inc(k_exped, 1)
            def mixed(t, k):
                act.wait_ge(mix_psum, t + 1)
                act.activation(K[:, bass.ds(t * D, D)], ps[0:P, 3 * k + 1, 0:D], ACT.Copy).then_inc(mix_copied, 1)

            with act.Fori(0, T // 2) as i:
                mixed(2 * i, 0)
                mixed(2 * i + 1, 1)
            mixed(T - 1, 0)
            act.wait_ge(var_ready, 2)
            act.activation(rstd, rstd, ACT.Sqrt).then_inc(std_ready, 1)

            act.wait_ge(gidx_ready, 1)
            with act.Fori(0, GTURNS) as i:
                for h in range(2):
                    act.wait_ge(chunk_summed, i * GU + GU // 2 * (h + 1))
                    apart(act)
                    copy(stage_gidx[h][:], gidx[:, bass.ds(i * GU + GU // 2 * h, GU // 2)]).then_inc(gidx_staged, 1)

            def router_copy(g, k, tiles):
                act.wait_ge(rT_psum, g + 1)
                n = tiles * DC
                copy(rxT[:, k, 0:n, :], ps[:, 4 + k, 0:n * P].rearrange("p (c n) -> p c n", n=P)).then_inc(rT_ready, 1)

            BEFORE = 2
            for g in range(2 * BEFORE):
                router_copy(g, g % 2, RP)
            act.wait_ge(var_ready, 3)
            act.activation(rstd, rstd, ACT.Sqrt).then_inc(std_ready, 1)
            with act.Fori(BEFORE, T // (2 * RP)) as i:
                router_copy(2 * i, 0, RP)
                router_copy(2 * i + 1, 1, RP)
            router_copy(T // RP, 0, T % RP)
            act.wait_ge(var_ready, 4)
            act.activation(probs, probs, ACT.Exp).then_inc(std_ready, 1)

            def xt_copy(j):
                act.wait_ge(xt_psum, j + 1)
                copy(XT, ps[:, 4, 0:DC * L].rearrange("p (c n) -> p c n", c=DC)).then_inc(xt_ready, 1)

            def do_silu(j):
                act.wait_ge(h_ready, j + 1)
                act.activation(silu, ps[:, 0:2, 0:HB], ACT.Silu).then_inc(silu_ready, 1)

            def round_wdn(experts):
                for e in experts:
                    at = slice(e * HC * D, (e + 1) * HC * D)
                    copy(wdn_high[:, at], wdn[:, at]).then_inc(wdn_rounded, 1)

            def gt_copy(j):
                act.wait_ge(gT_psum, j + 1)
                copy(GT_high[:, 0:4, :], ps[:, 5, :].rearrange("p (c n) -> p c n", n=L)).then_inc(gT_act, 1)

            act.wait_ge(pairs_placed, 1)
            act.wait_ge(s_wup, 16 * WPIECES)
            round_wdn(range(XP // 2))
            xt_copy(0)
            round_wdn(range(XP // 2, XP - 1))
            do_silu(0)
            xt_copy(1)
            round_wdn([XP - 1])
            gt_copy(0)
            with act.Fori(1, NBLK - 1) as j:
                do_silu(j)
                xt_copy(j + 1)
                gt_copy(j)
            do_silu(NBLK - 1)
            gt_copy(NBLK - 1)

        @block.tensor
        def _(pe):
            def bucket_map(turn, nb, blocks_n, reached, b0, b1):
                pe.matmul(ps[0:nb, b0, 0:1], count[:, 0:nb], ones[0:P, 0:1], start=True, stop=True)\
                  .then_inc(map_step, 1)
                pe.wait_ge(map_ready, 2 * turn + 1)
                pe.matmul(ps[0:nb, b1, 0:1], upper[0:nb, 0:nb], small_map[0:nb, 0:1], start=True, stop=True)\
                  .then_inc(map_step, 1)
                pe.wait_ge(map_ready, 2 * turn + 2)
                pe.matmul(ps[0:1, b0, 0:blocks_n], ones[0:nb, 0:1], reached, start=True, stop=True)\
                  .then_inc(map_step, 1)

            pe.wait_ge(s_const, 10)
            pe.wait_ge(count_ready, 1)
            pe.matmul(ps[0:P, 3, 0:T], upper[:], count, start=True, stop=True)
            pe.matmul(ps[:, 3, 32:32 + T], ones[0:P], count, start=True, stop=True).then_inc(base_ready, 1)

            def transpose_rows(bank, rows):
                for c in range(DC):
                    mm = pe.transpose(ps[:, bank, c * P:(c + 1) * P], rows[:, c * L:(c + 1) * L], ident[0:P, 0:P])
                return mm

            pe.sem_inc(xnT_psum, 2)
            pe.wait_ge(s_w, 16 * 6)

            def transpose_x(t, k):
                pe.wait_ge(xn_ready, t + 1)
                transpose_rows(3 * k, row_in[k]).then_inc(xnT_psum, 1)

            def project(t, k, more):
                if more:
                    transpose_x(t + 1, 1 - k)
                pe.wait_ge(xnT_ready, t + 1)
                pe.wait_ge(proj_free_act, t + 1)
                pe.wait_ge(proj_free_dve, t + 1)
                for n in range(2):
                    for c in range(DC):
                        mm = pe.matmul(ps[0:P, 3 * k + 1 + n, :], row_T[k][:, c, :], wqkvg[:, c, n * 512:(n + 1) * 512],
                                       start=(c == 0), stop=(c == DC - 1))
                mm.then_inc(proj_ready, 1)
                place_edges(t)

            def place_edges(t):
                for k in range(HK):
                    pe.wait_ge(edge_hot, (t * HK + k + 1) * 4)
                    pe.wait_ge(edge_scaled, (t * HK + k + 1) * 3)
                    for n in range(5):
                        mm = pe.matmul(ps[:, 6 + n // 3, 0:NCH], hot_row[n][:, k % NB, :], hot_chunk[:, k % NB, :],
                                       start=False, stop=False)
                    mm.then_inc(edges_placed, 1)

            def place_nothing(start):
                for bank in (6, 7):
                    mm = pe.matmul(ps[:, bank, 0:NCH], zero16, chunk_no16, start=start, stop=not start)
                return mm

            pe.sem_inc(edges_placed, NB)
            pe.wait_ge(parts_ready, 1)
            place_nothing(True)
            transpose_x(0, 0)
            with pe.Fori(0, T // 2) as i:
                project(2 * i, 0, True)
                project(2 * i + 1, 1, True)
            project(T - 1, 0, False)
            place_nothing(False).then_inc(edge_psum_ready, 1)
            pe.wait_ge(kmaxT_ready, 1)
            for c in range(DC):
                mm = pe.transpose(ps[:, 0, c * P:(c + 1) * P], kmax[:, c * L:(c + 1) * L], ident[0:P, 0:P])
            mm.then_inc(kmaxT_ready, 1)
            pe.wait_ge(kmaxb_ready, 1)
            for c in range(DC):
                mm = pe.matmul(ps[0:P, 1, c * L:(c + 1) * L], kmaxb[:, c, :], ident[:], start=True, stop=True)
            mm.then_inc(kshift_psum, 1)

            def context(t, start, stop):
                pe.wait_ge(k_exped, t + 1)
                for c in range(DC):
                    mm = pe.matmul(ps[:, 4 + c, 0:L + 1], K[:, t * D + c * L:t * D + (c + 1) * L],
                                   V[:, (t * DC + c) * (L + 1):(t * DC + c + 1) * (L + 1)], start=start, stop=stop)
                return mm

            for t in range(T):
                mm = context(t, t == 0, t == T - 1)
            mm.then_inc(ctx_ready, 1)
            pe.wait_ge(ctx_masked, 1)
            for c in range(DC):
                mm = pe.transpose(ps[:, 0, c * L:(c + 1) * L], context_sb[:, c, :], ident[:])
            mm.then_inc(ctx_ready, 1)
            pe.wait_ge(ctxT_ready, 1)
            for c in range(DC):
                mm = pe.matmul(ps[:, 1, c * D:(c + 1) * D], ctxT[:, c, :], wout_sb[:, c, :], start=True, stop=True)
            mm.then_inc(mixw_psum, 1)
            pe.wait_ge(mixw_ready, 1)

            def transpose_q(t, k):
                transpose_rows(3 * k, Q[:, t * D:(t + 1) * D]).then_inc(qT_psum, 1)

            def mix(t, k, more):
                if more:
                    transpose_q(t + 1, 1 - k)
                pe.wait_ge(qT_ready, t + 1)
                for c in range(DC):
                    mm = pe.matmul(ps[0:P, 3 * k + 1, 0:D], row_T[k][:, c, :], mix_w[:, c, :],
                                   start=(c == 0), stop=(c == DC - 1))
                mm.then_inc(mix_psum, 1)

            pe.wait_ge(q_ready, T)
            transpose_q(0, 0)
            for t in range(T):
                if t >= 2:
                    pe.wait_ge(mix_copied, t - 1)
                mix(t, t % 2, t + 1 < T)

            for c in range(DC):
                mm = pe.matmul(ps[:, 5, 256:256 + XP], ones[:], wr_sb[:, c, :], start=(c == 0), stop=(c == DC - 1))
            mm.then_inc(router_sum_ready, 1)
            bucket_map(0, T, NCH, chunk_reached, 2, 5)

            pe.sem_inc(chunk_summed, GU)
            with pe.Fori(0, GTURNS) as i:
                for k in range(GU):
                    pe.wait_ge(onehot_ready, i * GU + k + 1)
                    pe.wait_ge(gathered[k], 16 * (i + 1))
                    pe.wait_ge(chunk_added, i * GU + k + 1)
                    pe.matmul(ps[0:P, k % QK, 0:D], onehot[:, k, :], gbuf[:, k, :], start=True, stop=True)\
                        .then_inc(chunk_summed, 1)

            def tiles_of(g):
                return range(g * RP, min((g + 1) * RP, T))

            def transpose_x1(g):
                for t in tiles_of(g):
                    for c in range(DC):
                        at = ((t % RP) * DC + c) * P
                        mm = pe.transpose(ps[:, 4 + g % 2, at:at + P], acc[:, t, c * L:(c + 1) * L], ident[0:P, 0:P])
                mm.then_inc(rT_psum, 1)

            pe.wait_ge(x1_ready, 1)
            transpose_x1(0)
            for g in range(-(-T // RP)):
                if (g + 1) * RP < T:
                    transpose_x1(g + 1)
                pe.wait_ge(rT_ready, g + 1)
                for t in tiles_of(g):
                    for c in range(DC):
                        mm = pe.matmul(ps[0:P, 6, t * XP:(t + 1) * XP], rxT[:, g % 2, (t % RP) * DC + c, :],
                                       wr_sb[:, c, :], start=(c == 0), stop=(c == DC - 1))
                    mm.then_inc(logits_ready, 1)
            pe.wait_ge(pair_count_ready, 1)
            pe.matmul(ps[0:P, 7, 0:XP], upper[:], count[:, 0:XP], start=True, stop=True)
            pe.matmul(ps[:, 7, 32:32 + XP], ones[0:P], count[:, 0:XP], start=True, stop=True)\
              .then_inc(pair_base_ready, 1)

            for k in range(2):
                for t in range(T):
                    if t % PT == 0:
                        pe.wait_ge(pair_lanes_hot, k * len(pair_tiles) + t // PT + 1)
                        pe.wait_ge(pair_values_hot, k * len(pair_tiles) + t // PT + 1)
                    mm = pe.matmul(ps[:, 3, 0:2 * NBLK], lane_hot[k][:, t, :],
                                   block_hot[k][:, t, :, :].rearrange("p f j -> p (f j)"),
                                   start=(k == 0 and t == 0), stop=(k == 1 and t == T - 1))
            mm.then_inc(pairs_placed, 1)

            bucket_map(1, XP, NBLK, block_reached, 6, 7)

            pe.wait_ge(expert_map_ready, 1)
            pe.wait_ge(s_wup, 16 * WPIECES)

            def expert(j):
                return pe.value_load(block_expert[0:1, bass.ds(j, 1)], min_val=0, max_val=XP - 1)

            def x_transpose(j, k, turn):
                pe.wait_ge(x_loaded[k], 16 * turn)
                for c in range(DC):
                    mm = pe.transpose(ps[:, 4, c * L:(c + 1) * L], X[k][:, c * L:(c + 1) * L], ident[:])
                mm.then_inc(xt_psum, 1)

            def up(j, e):
                pe.wait_ge(xt_ready, j + 1)
                for n in range(4):
                    for c in range(DC):
                        mm = pe.matmul(ps[:, n, 0:HB], XT[:, c, :],
                                       wup[:, bass.ds(e * (DC * 2 * H) + (c * 2 * H + n * HB), HB)],
                                       start=(c == 0), stop=(c == DC - 1))
                mm.then_inc(h_ready, 1)

            def g_transpose(j):
                pe.wait_ge(g_ready, j + 1)
                for c in range(HC):
                    w = L if c < HC - 1 else HL
                    mm = pe.transpose(ps[0:w, 5 + c // 4, (c % 4) * L:(c % 4 + 1) * L], G[:, c * L:c * L + w], ident[:])
                mm.then_inc(gT_psum, 1)

            def down(j, e):
                pe.wait_ge(gT_act, j + 1)
                pe.wait_ge(gT_dve, 3 * (j + 1))
                parts = [(GT_low, wdn_high), (GT_high, wdn_low), (GT_high, wdn_high)]
                for n, (g, w) in enumerate(parts):
                    for c in range(HC):
                        rows = L if c < HC - 1 else HL
                        mm = pe.matmul(ps[:, 7, 0:D], g[0:rows, c, :], w[0:rows, bass.ds(e * (HC * D) + c * D, D)],
                                       start=(n == 0 and c == 0), stop=(n == 2 and c == HC - 1))
                mm.then_inc(y_psum, 1)

            def turn(j, k, loads, more, e, split=True):
                up(j, e)
                before = expert(j - 1)
                if more:
                    x_transpose(j + 1, 1 - k, loads)
                if not isinstance(j, int) or j >= 2:
                    pe.wait_ge(y_ready, j - 1)
                if not split:
                    pe.wait_ge(wdn_split, XP)
                down(j - 1, before)
                after = expert(j + 1) if more else e
                g_transpose(j)
                return after

            x_transpose(0, 0, 1)
            up(0, expert(0))
            x_transpose(1, 1, 1)
            g_transpose(0)
            e = turn(1, 1, 2, True, expert(1), split=False)
            turn(2, 0, 2, True, e)
            with pe.Fori(0, (NBLK - 4) // 4) as i:
                e = expert(4 * i + 3)
                for u in range(4):
                    e = turn(4 * i + 3 + u, (3 + u) % 2, 2 * i + 3 + u // 2, True, e)
            e = turn(NBLK - 1, 1, 0, False, expert(NBLK - 1))
            pe.wait_ge(y_ready, NBLK - 1)
            down(NBLK - 1, e)

        @block.vector
        def _(dve):
            v = nc.vector
            steps = Steps(dve, s_dve)
            v.memset(rank, 0.0).then_inc(s_dve, 1)
            v.memset(kmax, -3.0e38).then_inc(s_dve, 1)
            v.memset(context_sb, 0.0).then_inc(s_dve, 1)
            v.memset(V4[:, :, :, L], 1.0).then_inc(s_dve, 1)
            steps.n = 4
            dve.sem_inc(proj_free_dve, 2)
            dve.sem_inc(chunk_added, QK)

            dve.wait_ge(s_edges, 48)
            dve.wait_ge(s_const, 10)
            steps.link(v.tensor_scalar(tmp, src_i, 1.0 / T, -0.5 + 0.5 / T, ALU.mult, ALU.add))
            steps.link(v.tensor_scalar(row_of, tmp, ROUND, -ROUND, ALU.add, ALU.add))
            steps.link(v.scalar_tensor_tensor(tile_of16, row_of, -float(T), src_i, ALU.mult, ALU.add))
            steps.mark(v.scalar_tensor_tensor(rec.rearrange("p (c r) -> p c r", r=2)[:, :, 0], dst_i, float(ROW),
                                              row_of, ALU.mult, ALU.add))
            with steps.loop(0, T // GB, GB) as g:
                for k in range(GB):
                    b = g * GB + k
                    steps.mark(v.tensor_scalar(masks[:, bass.ds(b * 2 * MW, C)], tile_of16,
                                               tile_no[0:P, bass.ds(b, 1)], 0.0, ALU.is_equal, ALU.add,
                                               accum_out=count[:, bass.ds(b, 1)]))
            steps.wait()
            dve.sem_inc(count_ready, 1)

            def bucket_map(turn, nb, blocks_n, number, reached, out_i, b0, b1):
                dve.wait_ge(map_step, 3 * turn + 1)
                m = small_map
                steps.link(v.tensor_scalar(m[0:nb, 0:1], ps[0:nb, b0, 0:1], 1.0 / L, 0.5 - 0.5 / L, ALU.mult, ALU.add))
                steps.link(v.tensor_scalar(m[0:nb, 0:1], m[0:nb, 0:1], ROUND, -ROUND, ALU.add, ALU.add))
                dve.sem_inc(map_ready, 1)
                dve.wait_ge(map_step, 3 * turn + 2)
                steps.link(v.tensor_tensor(m[0:nb, 1:2], ps[0:nb, b1, 0:1], m[0:nb, 0:1], ALU.add))
                v.tensor_scalar(reached, number, m[0:nb, 1:2], None, ALU.is_ge).then_inc(map_ready, 1)
                dve.wait_ge(map_step, 3 * turn + 3)
                steps.link(v.tensor_scalar(out_i, ps[0:1, b0, 0:blocks_n], float(nb - 1), None, ALU.min))

            def block_counts(nb, bank):
                steps.link(v.tensor_scalar(blocks[:, 0:nb], ps[:, bank, 32:32 + nb], 1.0 / L, 0.5 - 0.5 / L,
                                           ALU.mult, ALU.add))
                steps.link(v.tensor_scalar(blocks[:, 0:nb], blocks[:, 0:nb], ROUND, -ROUND, ALU.add, ALU.add))
                steps.link(v.tensor_tensor_scan(blocks_to[:, 0:nb], blocks[:, 0:nb], blocks[:, 0:nb], 0.0,
                                                ALU.add, ALU.max))
                steps.link(v.tensor_tensor(first_slot[:, 0:nb], blocks_to[0:P, 0:nb], blocks[0:P, 0:nb], ALU.subtract))
                steps.link(v.scalar_tensor_tensor(first_slot[:, 0:nb], first_slot[:, 0:nb], float(L),
                                                  ps[0:P, bank, 0:nb], ALU.mult, ALU.add))

            dve.wait_ge(base_ready, 1)
            block_counts(T, 3)

            def slots(c0, c1):
                cols = slice(c0, c1)
                for b in range(T + 1):
                    if b < T:
                        steps.mark(v.tensor_tensor_scan(ps[0:P, 3 + b % GB, cols], mask[b][:, cols], mask[b][:, cols],
                                                        first_slot[:, b:b + 1], ALU.add, ALU.max))
                    if b > 0:
                        steps.wait(but=1 if b < T else 0)
                        counted = ps[0:P, 3 + (b - 1) % GB, :]
                        steps.mark(v.copy_predicated(rank[:, cols], mask[b - 1].bitcast(u16)[:, cols],
                                                     counted[:, cols]))
                        if c1 < C:
                            steps.mark(v.tensor_copy(first_slot[:, b - 1:b], counted[:, c1 - 1:c1]))
                steps.wait()
                steps.link(v.tensor_scalar(rank[:, cols], rank[:, cols], -1.0, None, ALU.add))
                steps.link(v.tensor_scalar(tmp[:, cols], rank[:, cols], 1.0 / L, -0.5 + 0.5 / L, ALU.mult, ALU.add))
                steps.link(v.tensor_scalar(tmp[:, cols], tmp[:, cols], ROUND, -ROUND, ALU.add, ALU.add))
                steps.link(v.scalar_tensor_tensor(tmp2[:, cols], tmp[:, cols], -float(L), rank[:, cols],
                                                  ALU.mult, ALU.add))
                v.scalar_tensor_tensor(slot_i[:, cols], tmp2[:, cols], float(NCH), tmp[:, cols],
                                       ALU.mult, ALU.add).then_inc(slots_ready, 1)

            slots(0, SFIRST * SU)
            slots(SFIRST * SU, C)

            steps.mark(v.tensor_copy(chunk_no16, chunk_no))
            steps.mark(v.tensor_copy(lane16, lane_row[0:P]))
            steps.mark(v.memset(zero16, 0.0))
            rest = wgt[:, C - PEC:C]
            for n in range(3):
                steps.link(v.tensor_copy(part16, rest))
                steps.link(v.tensor_copy(parts[:, n, :], part16))
                if n < 2:
                    left = row_of[:, n * PEC:(n + 1) * PEC]
                    steps.link(v.tensor_tensor(left, rest, parts[:, n, :], ALU.subtract))
                    rest = left
            number = rec.rearrange("p (c r) -> p c r", r=2)[:, C - PEC:C, 0]
            steps.link(v.tensor_scalar(parts[:, 3, :], number, 1.0 / LOW, -0.5 + 0.5 / LOW, ALU.mult, ALU.add))
            steps.link(v.tensor_scalar(parts[:, 3, :], parts[:, 3, :], ROUND, -ROUND, ALU.add, ALU.add))
            steps.link(v.tensor_scalar(parts[:, 3, :], parts[:, 3, :], LOW, None, ALU.mult))
            steps.link(v.tensor_tensor(parts[:, 4, :], number, parts[:, 3, :], ALU.subtract))
            dve.sem_inc(parts_ready, 1)

            dve.wait_ge(s_x, 16)
            dve.wait_ge(s_x2, 16)

            def tile_stats(t):
                return stats6[:, bass.ds(t * 6, 6)]

            def deviation(turn):
                steps.mark(v.tensor_tensor(mean, stats[:, :, 1], stats[:, :, 4], ALU.add))
                steps.mark(v.tensor_tensor(spread, stats[:, :, 1], stats[:, :, 4], ALU.subtract))
                steps.link(v.tensor_tensor(rstd, stats[:, :, 2], stats[:, :, 5], ALU.add))
                steps.mark(v.tensor_scalar(mean, mean, 0.5, None, ALU.mult))
                steps.mark(v.tensor_tensor(spread, spread, spread, ALU.mult))
                steps.link(v.tensor_scalar(rstd, rstd, 1.0 / D, EPS, ALU.mult, ALU.add))
                v.scalar_tensor_tensor(rstd, spread, 0.25, rstd, ALU.mult, ALU.add).then_inc(var_ready, 1)
                dve.wait_ge(std_ready, turn)
                steps.link(v.reciprocal(rstd, rstd))

            def acc_tile(t):
                return accf[:, bass.ds(t * D, D)]

            with steps.loop(0, T // GB, GB) as g:
                for r in range(GB):
                    steps.mark(v.bn_stats(tile_stats(g * GB + r), acc_tile(g * GB + r)))
            steps.wait()
            deviation(1)

            def by_head(a):
                return a.rearrange("p (h d) -> p h d", h=HEADS)

            def normalise(t, k):
                dve.wait_ge(xnT_psum, t + 1)
                v.tensor_scalar(row_in[k], acc_tile(t), mean[:, bass.ds(t, 1)], rstd[:, bass.ds(t, 1)],
                                ALU.subtract, ALU.mult).then_inc(xn_ready, 1)

            def q_divide(t):
                dve.wait_ge(q_exped, t + 1)
                apart(dve)
                qt = by_head(Q[:, bass.ds(t * D, D)])
                steps.link(v.tensor_reduce(qsum, qt, AX.X, ALU.add))
                steps.link(v.reciprocal(qrec, qsum))
                v.tensor_tensor(qt, qt, qrec.unsqueeze(2).broadcast_to([P, HEADS, DH]), ALU.mult).then_inc(q_ready, 1)

            def hot_edges(t):
                for k in range(HK):
                    dve.wait_ge(edges_placed, t * HK + k + 1)
                    c, row = t * HK + k, tmp2[:, bass.ds(C - PEC + t * HK + k, 1)]
                    v.tensor_scalar(hot_one[:, k % NB, :], lane16, row, None, ALU.is_equal).then_inc(edge_hot, 1)
                    v.tensor_scalar(hot_chunk[:, k % NB, :], chunk_no16, tmp[:, bass.ds(C - PEC + c, 1)], None,
                                    ALU.is_equal).then_inc(edge_hot, 1)
                    for n in range(2):
                        v.tensor_scalar(hot_row[n][:, k % NB, :], lane16, row, parts[:, n, bass.ds(c, 1)],
                                        ALU.is_equal, ALU.mult).then_inc(edge_hot, 1)

            def use_projections(t, k, before, more):
                if more:
                    normalise(t + 1, 1 - k)
                hot_edges(t)
                dve.wait_ge(proj_ready, t + 1)
                q, kk = ps[0:P, 3 * k + 2, 0:D], ps[0:P, 3 * k + 2, D:2 * D]
                steps.mark(v.tensor_reduce(qmax, by_head(q), AX.X, ALU.max))
                steps.link(v.tensor_copy(K[:, bass.ds(t * D, D)], kk))
                v.tensor_tensor(by_head(Q[:, bass.ds(t * D, D)]), by_head(q),
                                qmax.unsqueeze(2).broadcast_to([P, HEADS, DH]), ALU.subtract).then_inc(q_shifted, 1)
                steps.link(v.tensor_tensor(kmax, kk, kmax, ALU.max))
                dve.sem_inc(proj_free_dve, 1)
                if before:
                    q_divide(t - 1)

            normalise(0, 0)
            use_projections(0, 0, False, True)
            with steps.loop(0, T // 2 - 1, 10) as i:
                use_projections(2 * i + 1, 1, True, True)
                use_projections(2 * i + 2, 0, True, True)
            use_projections(T - 2, 1, True, True)
            use_projections(T - 1, 0, True, False)
            q_divide(T - 1)
            dve.sem_inc(kmaxT_ready, 1)

            dve.wait_ge(kmaxT_ready, 2)
            steps.link(v.tensor_reduce(kneg, ps[:, 0, 0:DC * P].rearrange("p (c n) -> p c n", c=DC), AX.X, ALU.max))
            v.tensor_copy(kmaxb, kneg.unsqueeze(2).broadcast_to([L, DC, P])).then_inc(kmaxb_ready, 1)
            dve.wait_ge(kshift_ready, 1)
            with dve.Fori(0, T // GB) as g:
                for r in range(GB):
                    kt = K[:, bass.ds((g * GB + r) * D, D)]
                    v.tensor_tensor(kt, kt, kshift, ALU.subtract).then_inc(k_shifted, 1)

            dve.wait_ge(ctx_ready, 1)
            for c in range(DC):
                for h in range(HPC):
                    r = slice(h * DH, (h + 1) * DH)
                    steps.mark(v.tensor_copy(context_sb[r, c, r], ps[r, 4 + c, r]))
            steps.wait()
            dve.sem_inc(ctx_masked, 1)
            for c in range(DC):
                steps.link(v.reciprocal(krec[:, c:c + 1], ps[:, 4 + c, L:L + 1]))
            dve.wait_ge(ctx_ready, 2)
            v.tensor_copy(ctxT, ps[:, 0, 0:DC * L].rearrange("p (c n) -> p c n", c=DC)).then_inc(ctxT_ready, 1)
            steps.link(v.tensor_scalar(krec, krec, SCALE, None, ALU.mult))
            dve.wait_ge(mixw_psum, 1)
            for c in range(DC):
                steps.mark(v.tensor_scalar(mix_w[:, c, :], ps[:, 1, c * D:(c + 1) * D], krec[:, c:c + 1], None,
                                           ALU.mult))
            steps.wait()
            steps.link(v.tensor_reduce(kneg, mix_w, AX.X, ALU.add))
            steps.link(v.tensor_scalar(kneg, kneg, 1.0 / D, None, ALU.mult))
            for c in range(DC):
                steps.mark(v.tensor_scalar(mix_w[:, c, :], mix_w[:, c, :], kneg[:, c:c + 1], None, ALU.subtract))
            steps.wait()
            dve.sem_inc(mixw_ready, 1)

            def attended(t, k, stats):
                dve.wait_ge(qT_psum, t + 1)
                v.tensor_copy(row_T[k], ps[:, 3 * k, 0:DC * P].rearrange("p (c n) -> p c n", c=DC))\
                 .then_inc(qT_ready, 1)
                if stats:
                    output_stats(t - 2)

            def output_stats(t):
                dve.wait_ge(mix_copied, t + 1)
                out = K[:, bass.ds(t * D, D)]
                steps.mark(v.bn_stats(tile_stats(t), out))
                steps.mark(v.tensor_tensor(out, out, gamma_sb, ALU.mult))

            attended(0, 0, False)
            attended(1, 1, False)
            with steps.loop(1, T // 2, 4) as i:
                attended(2 * i, 0, True)
                attended(2 * i + 1, 1, True)
            attended(T - 1, 0, True)
            output_stats(T - 2)
            output_stats(T - 1)
            steps.wait()
            deviation(2)
            with steps.loop(0, T // GB, GB) as g:
                for r in range(GB):
                    t = g * GB + r
                    steps.mark(v.scalar_tensor_tensor(acc_tile(t), K[:, bass.ds(t * D, D)], rstd[:, bass.ds(t, 1)],
                                                      acc_tile(t), ALU.mult, ALU.add))
            steps.wait()

            bucket_map(0, T, NCH, chunk_no[0:T], chunk_reached, chunk_tile[:], 2, 5)

            dve.wait_ge(router_sum_ready, 1)
            for c in range(DC):
                steps.mark(v.scalar_tensor_tensor(wr_sb[:, c, :], ps[:, 5, 256:256 + XP], -1.0 / D, wr_sb[:, c, :],
                                                  ALU.mult, ALU.add))
            steps.wait()

            dve.wait_ge(s_recs, 16)
            dve.wait_ge(s_support_out, 32)
            dve.wait_ge(edge_psum_ready, 1)
            both_numbers = rec_in.rearrange("p (c r) -> p c r", r=2)
            first_number = both_numbers[:, :, 0]
            steps.link(v.tensor_tensor(first_number, first_number, ps[:, 7, 0:NCH], ALU.add))
            steps.link(v.tensor_scalar(edge_target, first_number, 1.0 / ROW, -0.5 + 0.5 / ROW, ALU.mult, ALU.add))
            steps.link(v.tensor_scalar(edge_target, edge_target, ROUND, -ROUND, ALU.add, ALU.add))
            v.tensor_copy(gidx, edge_target).then_inc(gidx_ready, 1)
            steps.mark(v.tensor_tensor(both_numbers[:, :, 1], both_numbers[:, :, 1], ps[:, 6, 0:NCH], ALU.add))
            steps.link(v.scalar_tensor_tensor(edge_row, edge_target, -float(ROW), first_number, ALU.mult, ALU.add))

            def edge_rows_of(c, k):
                v.tensor_scalar(onehot[:, k, :], lane_no, edge_row[:, bass.ds(c, 1)],
                                rec_in[:, bass.ds(c * 2 + 1, 1)], ALU.is_equal, ALU.mult).then_inc(onehot_ready, 1)

            def add_blocks(i, more):
                _, tiles = nc.values_load_multi_w_load_instructions(
                    chunk_tile[0:1, bass.ds(i * GU, GU)], engines=(mybir.EngineType.DVE,), min_val=0, max_val=T - 1)
                for k in range(GU):
                    dve.wait_ge(chunk_summed, GU + i * GU + k + 1)
                    a = accf[:, bass.ds(tiles[k] * D, D)]
                    v.tensor_tensor(a, a, ps[0:P, k % QK, 0:D], ALU.add).then_inc(chunk_added, 1)
                    if more:
                        edge_rows_of((i + 1) * GU + k, k)
                    dve.wait_ge(chunk_added, QK + i * GU + k + 1)

            for k in range(GU):
                edge_rows_of(k, k)
            with dve.Fori(0, GTURNS - 1) as i:
                add_blocks(i, True)
            add_blocks(GTURNS - 1, False)
            dve.sem_inc(x1_ready, 1)

            with steps.loop(0, T // GB, GB) as g:
                for r in range(GB):
                    steps.mark(v.bn_stats(tile_stats(g * GB + r), acc_tile(g * GB + r)))
            steps.wait()
            deviation(3)

            with dve.Fori(0, T // GB) as g:
                for r in range(GB):
                    t = g * GB + r
                    v.tensor_scalar(normf[:, bass.ds(t * D, D)], acc_tile(t), mean[:, bass.ds(t, 1)],
                                    rstd[:, bass.ds(t, 1)], ALU.subtract, ALU.mult).then_inc(norm_ready, 1)
            dve.wait_ge(logits_ready, T)
            lg = ps[0:P, 6, 0:TX].rearrange("p (t e) -> p t e", e=XP)

            def over_experts(a):
                return a.unsqueeze(2).broadcast_to([P, T, XP])

            def over_tiles(a):
                return a.unsqueeze(1).broadcast_to([P, T, XP])

            steps.link(v.tensor_tensor(logits, lg, over_experts(rstd), ALU.mult))
            steps.link(v.tensor_reduce(r1[0], logits, AX.X, ALU.max))
            v.tensor_tensor(probs, logits, over_experts(r1[0]), ALU.subtract).then_inc(var_ready, 1)
            dve.wait_ge(std_ready, 4)
            steps.link(v.tensor_reduce(r1[0], probs, AX.X, ALU.add))
            steps.link(v.reciprocal(r1[1], r1[0]))
            steps.link(v.tensor_tensor(probs, probs, over_experts(r1[1]), ALU.mult))

            def pick(mine, top):
                steps.link(v.tensor_reduce(top, probs, AX.X, ALU.max))
                steps.link(v.tensor_tensor(key, probs, over_experts(top), ALU.is_equal))
                steps.link(v.tensor_tensor(key, key, over_tiles(expert_rev[:]), ALU.mult))
                steps.link(v.tensor_reduce(r1[0], key, AX.X, ALU.max))
                steps.link(v.tensor_tensor(mine, key, over_experts(r1[0]), ALU.is_equal))

            pick(first, r1[1])
            steps.link(v.scalar_tensor_tensor(probs, first, -2.0, probs, ALU.mult, ALU.add))
            pick(second, r1[2])
            steps.link(v.tensor_tensor(r1[0], r1[1], r1[2], ALU.add))
            steps.link(v.tensor_scalar(r1[0], r1[0], 1e-9, None, ALU.add))
            steps.link(v.reciprocal(r1[3], r1[0]))
            steps.mark(v.tensor_tensor(gate[:, 0, :], r1[1], r1[3], ALU.mult))
            steps.mark(v.tensor_tensor(gate[:, 1, :], r1[2], r1[3], ALU.mult))
            steps.wait()
            steps.link(v.tensor_tensor(both, first, second, ALU.add))
            for e in range(XP):
                steps.mark(v.tensor_tensor_scan(cum[:, :, e], both[:, :, e], both[:, :, e], 0.0, ALU.add, ALU.max))
            steps.wait()
            v.tensor_copy(count[:, 0:XP], cum[:, T - 1, :]).then_inc(pair_count_ready, 1)
            dve.wait_ge(pair_base_ready, 1)
            block_counts(XP, 7)
            steps.link(v.tensor_scalar(first_slot[:, 0:XP], first_slot[:, 0:XP], -1.0, None, ALU.add))
            steps.link(v.tensor_tensor(place, cum, over_tiles(first_slot[:, 0:XP]), ALU.add))
            dve.wait_ge(norm_out, 16 * 2 * (T // GB))
            dve.wait_ge(x1_out, 32)
            for k, mine in enumerate((first, second)):
                steps.mark(v.tensor_tensor(keys[k], mine, place, ALU.mult))
            steps.wait()
            for k in range(2):
                steps.mark(v.tensor_reduce(pair_slot[:, k, :], keys[k], AX.X, ALU.add))
            steps.wait()
            steps.link(v.tensor_scalar(pair_block, pair_slot, 1.0 / L, -0.5 + 0.5 / L, ALU.mult, ALU.add))
            steps.link(v.tensor_scalar(pair_block, pair_block, ROUND, -ROUND, ALU.add, ALU.add))
            steps.link(v.scalar_tensor_tensor(pair_slot, pair_block, -float(L), pair_slot, ALU.mult, ALU.add))
            for k in range(2):
                for at in pair_tiles:
                    n = at.stop - at.start
                    v.tensor_tensor(block_hot[k][:, at, 0, :], block_no.unsqueeze(1).broadcast_to([P, n, NBLK]),
                                    pair_block[:, k, at].unsqueeze(2).broadcast_to([P, n, NBLK]), ALU.is_equal)\
                     .then_inc(pair_blocks_hot, 1)
                    v.tensor_tensor(lane_hot[k][:, at, :], lane_row[0:P].unsqueeze(1).broadcast_to([P, n, L]),
                                    pair_slot[:, k, at].unsqueeze(2).broadcast_to([P, n, L]), ALU.is_equal)\
                     .then_inc(pair_lanes_hot, 1)
            dve.wait_ge(pairs_placed, 1)
            steps.mark(v.tensor_copy(block_gate, ps[:, 3, NBLK:2 * NBLK]))
            steps.link(v.tensor_scalar(block_node, ps[:, 3, 0:NBLK], -1.0, None, ALU.add))
            steps.mark(v.tensor_scalar(block_empty, block_node, 0.0, float(N + 1), ALU.is_lt, ALU.mult))
            steps.link(v.tensor_scalar(block_token, block_node, 0.0, None, ALU.max))
            steps.link(v.tensor_tensor(block_node, block_node, block_empty, ALU.add))
            steps.link(v.tensor_scalar(block_empty, block_empty, 1.0 / (N + 1), lane, ALU.mult, ALU.mult))
            v.tensor_tensor(block_dest, block_node, block_empty, ALU.add).then_inc(blocks_ready, 1)
            bucket_map(1, XP, NBLK, block_no[0:XP], block_reached, block_expert[:], 6, 7)
            dve.sem_inc(expert_map_ready, 1)

            def gated(j):
                dve.wait_ge(silu_ready, j + 1)
                v.tensor_tensor(G.rearrange("p (a n) -> p a n", a=2), ps[:, 2:4, 0:HB], silu, ALU.mult)\
                 .then_inc(g_ready, 1)

            def gt_copy(j):
                dve.wait_ge(gT_psum, j + 1)
                last, left = ps[:, 6, 0:L], ps[0:HL, 6, L:2 * L]
                steps.mark(v.tensor_copy(GT_high[:, 4, :], last))
                steps.mark(v.tensor_copy(GT_high[0:HL, 5, :], left))
                dve.wait_ge(gT_act, j + 1)
                v.tensor_tensor(GT_low[:, 0:4, :], ps[:, 5, :].rearrange("p (c n) -> p c n", n=L), GT_high[:, 0:4, :],
                                ALU.subtract).then_inc(gT_dve, 1)
                steps.wait()
                v.tensor_tensor(GT_low[:, 4, :], last, GT_high[:, 4, :], ALU.subtract).then_inc(gT_dve, 1)
                v.tensor_tensor(GT_low[0:HL, 5, :], left, GT_high[0:HL, 5, :], ALU.subtract).then_inc(gT_dve, 1)

            def y_copy(j, k, first):
                dve.wait_ge(y_psum, j + 1)
                if not first:
                    dve.wait_ge(y_added, 16 * (j - 1))
                v.tensor_scalar(Y[k], ps[:, 7, 0:D], block_gate[:, bass.ds(j, 1)], None, ALU.mult)\
                 .then_inc(y_ready, 1)

            def turn(j, k, first):
                gated(j)
                y_copy(j - 1, 1 - k, first)
                gt_copy(j)

            split_wdn(v, [0, 1, 2, 3, 6])
            gated(0)
            split_wdn(v, [7])
            gt_copy(0)
            turn(1, 1, True)
            turn(2, 0, True)
            with steps.loop(1, NBLK // 2 - 1, 4) as i:
                turn(2 * i + 1, 1, False)
                turn(2 * i + 2, 0, False)
            turn(NBLK - 1, 1, False)
            y_copy(NBLK - 1, 1, False)


def kernel(x, src, dst, edge_weight, L0_gnn_W, L0_mix_Wqkv, L0_mix_Wout, L0_mix_gamma,
           L0_ffn_router_w, L0_ffn_w1, L0_ffn_w2, L0_ffn_w3):
    import numpy as np
    import concourse.bacc as _bacc
    from concourse import mybir as _mybir
    from concourse.bass_utils import run_bass_kernel_spmd as _run

    L = 128
    N, D = x.shape
    E = src.shape[0]
    XP, H, _ = L0_ffn_w1.shape
    HC = -(-H // L)
    T = 25
    w1, w2, w3 = (np.asarray(a) for a in (L0_ffn_w1, L0_ffn_w2, L0_ffn_w3))
    w_up = np.concatenate([w1, w3], axis=1).transpose(2, 0, 1).reshape(D // L, L, XP, 2 * H).transpose(1, 2, 0, 3)
    w_down = np.zeros((XP, HC * L, D), w2.dtype)
    w_down[:, :H, :] = w2.transpose(0, 2, 1)
    w_down = w_down.reshape(XP, HC, L, D).transpose(2, 0, 1, 3)
    ins = {
        "x": np.asarray(x), "src": np.asarray(src), "dst": np.asarray(dst), "edge_weight": np.asarray(edge_weight),
        "w_gnn": np.asarray(L0_gnn_W), "w_qkv": np.asarray(L0_mix_Wqkv), "w_out": np.asarray(L0_mix_Wout),
        "gamma": np.broadcast_to(np.asarray(L0_mix_gamma), (N // T, D)), "w_router": np.asarray(L0_ffn_router_w).T,
        "w_up": w_up, "w_down": w_down,
    }
    nc = _bacc.Bacc("TRN2", target_bir_lowering=False, num_devices=1)
    f32 = _mybir.dt.float32
    arrays, args = {}, []
    for name, a in ins.items():
        a = np.ascontiguousarray(a)
        arrays[f"in_{name}"] = a
        args.append(nc.dram_tensor(f"in_{name}", a.shape, _mybir.dt.from_np(a.dtype), kind="ExternalInput").ap())
    args.append(nc.dram_tensor("x_out", (N + L, D), f32, kind="ExternalOutput").ap())
    chunks = -(-((E + T * (L - 1)) // L) // 8) * 8
    args.append(nc.dram_tensor("support_table", (N, D), f32, kind="Internal").ap())
    args.append(nc.dram_tensor("edge_table", (L * chunks, 2), f32, kind="Internal").ap())
    args.append(nc.dram_tensor("norm_table", (N, D), f32, kind="Internal").ap())
    gps_layer_program(nc, *args)
    r = _run(nc, [arrays], core_ids=[0])
    return r.results[0]["x_out"][:N]
```
